# Optimizing a Trainium2 kernel written in Bass

```python
import numpy as np
import jax
import jax.numpy as jnp

def _softmax(x, axis=-1):
    return jax.nn.softmax(x, axis=axis)

def _gelu(x):
    return jax.nn.gelu(x, approximate=True)

def _silu(x):
    return jax.nn.silu(x)

def _sigmoid(x):
    return jax.nn.sigmoid(x)

def _layernorm(x, axis=-1, eps=1e-05):
    m = jnp.mean(x, axis=axis, keepdims=True)
    v = jnp.var(x, axis=axis, keepdims=True)
    return (x - m) / jnp.sqrt(v + eps)

def _scatter_add(tgt, idx, src, axis=0):
    return tgt.at[idx].add(src)

def _segment_sum(src, seg, n):
    return jax.ops.segment_sum(src, seg, n)
kernel_name = 'mk_hybrid_d1_jaxref_r4_ea63a3'

def setup_inputs(seed: int=0):
    np.random.seed(seed)
    _w = jnp.asarray

    def _L0_attn_a_setup():
        import jax, jax.numpy as jnp
        import numpy as np
        B_, L_, D_, N_ = (4, 1024, 256, 32)
        key = jax.random.key(seed)
        ks = jax.random.split(key, 8)

        def n(k, shape, s=0.02):
            return jax.random.normal(k, shape, jnp.float32) * s
        return {'x': jax.random.normal(ks[0], (B_, L_, D_), jnp.float32), 'in_w': n(ks[1], (2 * D_, D_)), 'in_b': jnp.zeros((2 * D_,), jnp.float32), 'conv_w': n(ks[2], (D_, 1, 4), 0.1), 'conv_b': jnp.zeros((D_,), jnp.float32), 'A_log': -2.0 + 0.1 * jax.random.normal(ks[3], (D_, N_), jnp.float32), 'B_w': n(ks[4], (N_, D_)), 'B_b': jnp.zeros((N_,), jnp.float32), 'C_w': n(ks[5], (N_, D_)), 'C_b': jnp.zeros((N_,), jnp.float32), 'out_w': n(ks[6], (D_, D_)), 'out_b': jnp.zeros((D_,), jnp.float32), 'ln_w': jnp.ones((D_,), jnp.float32), 'ln_b': jnp.zeros((D_,), jnp.float32)}
    _L0_attn_a_in = _L0_attn_a_setup()

    def _L0_attn_b_setup():
        import jax, jax.numpy as jnp
        import numpy as np
        B, S, D, H, MLP = (2, 512, 256, 16, 1024)
        DH = D // H
        EPS_LN = 1e-06
        KERNEL_EPS = 0.001

        def layer_norm(x, scale, bias):
            m = jnp.mean(x, axis=-1, keepdims=True)
            v = jnp.mean(jnp.square(x - m), axis=-1, keepdims=True)
            return (x - m) * jax.lax.rsqrt(v + EPS_LN) * scale + bias

        def performer_causal_attention(q, k, v):
            phi_q = jax.nn.relu(q) + KERNEL_EPS
            phi_k = jax.nn.relu(k) + KERNEL_EPS
            kv = jnp.cumsum(jnp.einsum('bshm,bshd->bshmd', phi_k, v), axis=1)
            num = jnp.einsum('bshm,bshmd->bshd', phi_q, kv)
            den = jnp.einsum('bshm,bshm->bsh', phi_q, jnp.cumsum(phi_k, axis=1))
            return num / den[..., None]
        key = jax.random.key(seed)
        ks = jax.random.split(key, 7)

        def w(k, shape, scale):
            return jax.random.normal(k, shape, jnp.float32) * scale
        s_in = 1.0 / np.sqrt(D)
        return {'inputs': jax.random.normal(ks[0], (B, S, D), jnp.float32), 'ln1_scale': jnp.ones((D,), jnp.float32), 'ln1_bias': jnp.zeros((D,), jnp.float32), 'wq': w(ks[1], (D, H, DH), s_in), 'wk': w(ks[2], (D, H, DH), s_in), 'wv': w(ks[3], (D, H, DH), s_in), 'wo': w(ks[4], (H, DH, D), s_in), 'ln2_scale': jnp.ones((D,), jnp.float32), 'ln2_bias': jnp.zeros((D,), jnp.float32), 'w1': w(ks[5], (D, MLP), s_in), 'b1': jnp.zeros((MLP,), jnp.float32), 'w2': w(ks[6], (MLP, D), 1.0 / np.sqrt(MLP)), 'b2': jnp.zeros((D,), jnp.float32)}
    _L0_attn_b_in = _L0_attn_b_setup()

    def _L0_ffn_setup():
        import jax, jax.numpy as jnp
        import numpy as np
        D_MODEL = 256
        EXPERT_DIM = 256
        NUM_EXPERTS = 8
        TOP_K = 2
        B, T = (8, 1024)
        key = jax.random.key(seed)
        ks = jax.random.split(key, 5)
        scale_in = 1.0 / np.sqrt(D_MODEL)
        scale_h = 1.0 / np.sqrt(EXPERT_DIM)
        return {'x': jax.random.normal(ks[0], (B, T, D_MODEL), dtype=jnp.float32), 'gate_w': jax.random.normal(ks[1], (D_MODEL, NUM_EXPERTS), dtype=jnp.float32) * scale_in, 'gate_b': jnp.zeros((NUM_EXPERTS,), dtype=jnp.float32), 'w1': jax.random.normal(ks[2], (NUM_EXPERTS, D_MODEL, EXPERT_DIM), dtype=jnp.float32) * scale_in, 'b1': jnp.zeros((NUM_EXPERTS, EXPERT_DIM), dtype=jnp.float32), 'w2': jax.random.normal(ks[3], (NUM_EXPERTS, EXPERT_DIM, D_MODEL), dtype=jnp.float32) * scale_h, 'b2': jnp.zeros((NUM_EXPERTS, D_MODEL), dtype=jnp.float32)}
    _L0_ffn_in = _L0_ffn_setup()
    _d = {'L0_attn_a_x': _L0_attn_a_in['x'], 'L0_attn_a_in_w': _L0_attn_a_in['in_w'], 'L0_attn_a_in_b': _L0_attn_a_in['in_b'], 'L0_attn_a_conv_w': _L0_attn_a_in['conv_w'], 'L0_attn_a_conv_b': _L0_attn_a_in['conv_b'], 'L0_attn_a_A_log': _L0_attn_a_in['A_log'], 'L0_attn_a_B_w': _L0_attn_a_in['B_w'], 'L0_attn_a_B_b': _L0_attn_a_in['B_b'], 'L0_attn_a_C_w': _L0_attn_a_in['C_w'], 'L0_attn_a_C_b': _L0_attn_a_in['C_b'], 'L0_attn_a_out_w': _L0_attn_a_in['out_w'], 'L0_attn_a_out_b': _L0_attn_a_in['out_b'], 'L0_attn_a_ln_w': _L0_attn_a_in['ln_w'], 'L0_attn_a_ln_b': _L0_attn_a_in['ln_b'], 'L0_attn_b_ln1_scale': _L0_attn_b_in['ln1_scale'], 'L0_attn_b_ln1_bias': _L0_attn_b_in['ln1_bias'], 'L0_attn_b_wq': _L0_attn_b_in['wq'], 'L0_attn_b_wk': _L0_attn_b_in['wk'], 'L0_attn_b_wv': _L0_attn_b_in['wv'], 'L0_attn_b_wo': _L0_attn_b_in['wo'], 'L0_attn_b_ln2_scale': _L0_attn_b_in['ln2_scale'], 'L0_attn_b_ln2_bias': _L0_attn_b_in['ln2_bias'], 'L0_attn_b_w1': _L0_attn_b_in['w1'], 'L0_attn_b_b1': _L0_attn_b_in['b1'], 'L0_attn_b_w2': _L0_attn_b_in['w2'], 'L0_attn_b_b2': _L0_attn_b_in['b2'], 'L0_ffn_gate_w': _L0_ffn_in['gate_w'], 'L0_ffn_gate_b': _L0_ffn_in['gate_b'], 'L0_ffn_w1': _L0_ffn_in['w1'], 'L0_ffn_b1': _L0_ffn_in['b1'], 'L0_ffn_w2': _L0_ffn_in['w2'], 'L0_ffn_b2': _L0_ffn_in['b2']}
    _x0 = _d['L0_attn_a_x']
    _d['L0_attn_a_x'] = jax.random.normal(jax.random.fold_in(jax.random.key(seed), 1), (4, 1024, 256), dtype=_x0.dtype)
    del _x0
    return _d

def reference(L0_attn_a_x, L0_attn_a_in_w, L0_attn_a_in_b, L0_attn_a_conv_w, L0_attn_a_conv_b, L0_attn_a_A_log, L0_attn_a_B_w, L0_attn_a_B_b, L0_attn_a_C_w, L0_attn_a_C_b, L0_attn_a_out_w, L0_attn_a_out_b, L0_attn_a_ln_w, L0_attn_a_ln_b, L0_attn_b_ln1_scale, L0_attn_b_ln1_bias, L0_attn_b_wq, L0_attn_b_wk, L0_attn_b_wv, L0_attn_b_wo, L0_attn_b_ln2_scale, L0_attn_b_ln2_bias, L0_attn_b_w1, L0_attn_b_b1, L0_attn_b_w2, L0_attn_b_b2, L0_ffn_gate_w, L0_ffn_gate_b, L0_ffn_w1, L0_ffn_b1, L0_ffn_w2, L0_ffn_b2):

    def _L0_attn_a_ref(x, in_w, in_b, conv_w, conv_b, A_log, B_w, B_b, C_w, C_b, out_w, out_b, ln_w, ln_b):
        import jax, jax.numpy as jnp
        import numpy as np
        B_, L_, D_, N_ = (4, 1024, 256, 32)
        Bsz, L, D = x.shape
        residual = x
        xz = x @ in_w.T + in_b
        xa, z = (xz[..., :D], xz[..., D:])
        xc = jax.lax.conv_general_dilated(xa.transpose(0, 2, 1), conv_w, (1,), [(2, 2)], feature_group_count=D, dimension_numbers=('NCH', 'OIH', 'NCH'))
        xc = xc + conv_b[None, :, None]
        xc = jax.nn.silu(xc.transpose(0, 2, 1))
        A = -jnp.exp(jnp.clip(A_log, -5.0, 2.0))
        Bm = xc @ B_w.T + B_b
        Cm = xc @ C_w.T + C_b
        xs = (xc[:, :L].transpose(1, 0, 2), Bm[:, :L].transpose(1, 0, 2), Cm[:, :L].transpose(1, 0, 2))
        s0 = jnp.zeros((Bsz, D, A.shape[1]), x.dtype)

        def step(s, t):
            x_t, b_t, c_t = t
            s = jnp.clip(s * A + b_t[:, None, :] * x_t[:, :, None], -10.0, 10.0)
            y = jnp.sum(c_t[:, None, :] * s, axis=-1)
            return (s, y)
        _, ys = jax.lax.scan(step, s0, xs)
        y = ys.transpose(1, 0, 2) * jax.nn.silu(z)
        out = y @ out_w.T + out_b
        h = out + residual
        mu = jnp.mean(h, axis=-1, keepdims=True)
        var = jnp.var(h, axis=-1, keepdims=True)
        return (h - mu) / jnp.sqrt(var + 1e-05) * ln_w + ln_b

    def _L0_attn_b_ref(inputs, ln1_scale, ln1_bias, wq, wk, wv, wo, ln2_scale, ln2_bias, w1, b1, w2, b2):
        import jax, jax.numpy as jnp
        import numpy as np
        B, S, D, H, MLP = (2, 512, 256, 16, 1024)
        DH = D // H
        EPS_LN = 1e-06
        KERNEL_EPS = 0.001

        def layer_norm(x, scale, bias):
            m = jnp.mean(x, axis=-1, keepdims=True)
            v = jnp.mean(jnp.square(x - m), axis=-1, keepdims=True)
            return (x - m) * jax.lax.rsqrt(v + EPS_LN) * scale + bias

        def performer_causal_attention(q, k, v):
            phi_q = jax.nn.relu(q) + KERNEL_EPS
            phi_k = jax.nn.relu(k) + KERNEL_EPS
            kv = jnp.cumsum(jnp.einsum('bshm,bshd->bshmd', phi_k, v), axis=1)
            num = jnp.einsum('bshm,bshmd->bshd', phi_q, kv)
            den = jnp.einsum('bshm,bshm->bsh', phi_q, jnp.cumsum(phi_k, axis=1))
            return num / den[..., None]
        x = layer_norm(inputs, ln1_scale, ln1_bias)
        q = jnp.einsum('bsd,dhm->bshm', x, wq)
        k = jnp.einsum('bsd,dhm->bshm', x, wk)
        v = jnp.einsum('bsd,dhm->bshm', x, wv)
        attn = performer_causal_attention(q, k, v)
        attn_out = jnp.einsum('bshm,hmd->bsd', attn, wo)
        x = attn_out + inputs
        y = layer_norm(x, ln2_scale, ln2_bias)
        y = jax.nn.gelu(y @ w1 + b1) @ w2 + b2
        return x + y

    def _L0_ffn_ref(x, gate_w, gate_b, w1, b1, w2, b2):
        import jax, jax.numpy as jnp
        import numpy as np
        D_MODEL = 256
        EXPERT_DIM = 256
        NUM_EXPERTS = 8
        TOP_K = 2
        B, T = (8, 1024)
        b, t, d = x.shape
        xf = x.reshape(b * t, d)
        scores = xf @ gate_w + gate_b
        topk_s, topk_i = jax.lax.top_k(scores, TOP_K)
        n = xf.shape[0]
        comb = jnp.zeros_like(scores).at[jnp.arange(n)[:, None], topk_i].add(topk_s)
        h = jnp.maximum(jnp.einsum('nd,edh->neh', xf, w1) + b1, 0.0)
        eo = jnp.einsum('neh,ehd->ned', h, w2) + b2
        out = jnp.einsum('ne,ned->nd', comb, eo)
        return out.reshape(b, t, d)
    x = L0_attn_a_x
    x = x + _L0_attn_a_ref(_layernorm(x, axis=-1), L0_attn_a_in_w, L0_attn_a_in_b, L0_attn_a_conv_w, L0_attn_a_conv_b, L0_attn_a_A_log, L0_attn_a_B_w, L0_attn_a_B_b, L0_attn_a_C_w, L0_attn_a_C_b, L0_attn_a_out_w, L0_attn_a_out_b, L0_attn_a_ln_w, L0_attn_a_ln_b)
    x = x + _L0_ffn_ref(_layernorm(x, axis=-1), L0_ffn_gate_w, L0_ffn_gate_b, L0_ffn_w1, L0_ffn_b1, L0_ffn_w2, L0_ffn_b2)
    x = x + _L0_attn_b_ref(_layernorm(x, axis=-1), L0_attn_b_ln1_scale, L0_attn_b_ln1_bias, L0_attn_b_wq, L0_attn_b_wk, L0_attn_b_wv, L0_attn_b_wo, L0_attn_b_ln2_scale, L0_attn_b_ln2_bias, L0_attn_b_w1, L0_attn_b_b1, L0_attn_b_w2, L0_attn_b_b2)
    x = x + _L0_ffn_ref(_layernorm(x, axis=-1), L0_ffn_gate_w, L0_ffn_gate_b, L0_ffn_w1, L0_ffn_b1, L0_ffn_w2, L0_ffn_b2)
    return x

_drawn_inputs = setup_inputs


def setup_inputs(seed=0):
    import zlib

    import numpy as np

    out = dict(_drawn_inputs(seed))
    spreads = {'L0_attn_a_in_b': (0.0, 0.8),
     'L0_attn_a_conv_b': (0.0, 0.8),
     'L0_attn_a_B_b': (0.0, 0.8),
     'L0_attn_a_C_b': (0.0, 0.8),
     'L0_attn_a_out_b': (0.0, 2.0),
     'L0_attn_a_ln_w': (1.0, 0.2),
     'L0_attn_a_ln_b': (0.0, 0.1),
     'L0_attn_b_ln1_scale': (1.0, 0.6),
     'L0_attn_b_ln1_bias': (0.0, 0.1),
     'L0_attn_b_ln2_scale': (1.0, 0.2),
     'L0_attn_b_ln2_bias': (0.0, 0.1),
     'L0_attn_b_b1': (0.0, 0.1),
     'L0_attn_b_b2': (0.0, 0.1),
     'L0_ffn_gate_b': (0.0, 0.1),
     'L0_ffn_b1': (0.0, 0.1),
     'L0_ffn_b2': (0.0, 0.1)}
    factors = {'L0_attn_a_in_w': 8.0,
     'L0_attn_a_conv_w': 8.0,
     'L0_attn_a_A_log': 8.0,
     'L0_attn_a_B_w': 8.0,
     'L0_attn_a_C_w': 8.0,
     'L0_attn_a_out_w': 8.0}
    for name, (base, spread) in spreads.items():
        noise = np.random.default_rng([zlib.crc32(name.encode()), seed]).standard_normal(out[name].shape)
        drawn = base * np.exp(spread * noise) if base else spread * noise
        out[name] = jnp.asarray(drawn.astype(out[name].dtype))
    for name, factor in factors.items():
        out[name] = (out[name] * factor).astype(out[name].dtype)
    return out
```

```python
import numpy as np
import concourse.bass as bass
from concourse import mybir
from contextlib import ExitStack

B, L, D = 4, 1024, 256
N_STATE = 32
TAPS = 4
H, DH = 16, 16
MLP = 1024
E, F = 8, 256
P = 128
KD = D // P
CT = 64
CHUNKS = L // CT
TILES = B * CT // P
TOK = B * CT
QUARTERS = 4
QT = CT // QUARTERS
PAIRS = CT // 2
YSTEPS = 8
YROWS = YSTEPS * B
RING = 8
SPLITS = 4
ROWS = SPLITS * B
PADH = 32
GROUPS = H * PADH // P
GH = H // GROUPS
HV = DH + 1
LIMIT = 10.0
KERNEL_EPS = 0.001
HALF = D // 2


def constants():
    p = np.arange(P)
    ident = np.eye(P, dtype=np.float32)
    same = (p[:, None] // CT) == (p[None, :] // CT)
    causal = (same & (p[:, None] <= p[None, :])).astype(np.float32)
    own_head = np.zeros((P, GROUPS, GH, HV), np.float32)
    for hh in range(GH):
        own_head[PADH * hh:PADH * hh + DH, :, hh, :] = 1.0
    feature_eps = np.where(p % PADH < DH, KERNEL_EPS, 0.0).astype(np.float32)[:, None]
    own_batch = (p[:, None] // N_STATE == np.arange(B)[None, :]).astype(np.float32)
    before = np.tile((np.arange(E)[None, :] < np.arange(E)[:, None]).astype(np.float32)[None], (P, 1, 1))
    return {
        "ident": ident, "causal": causal, "own_head": own_head.reshape(P, -1),
        "feature_eps": feature_eps, "own_batch": own_batch, "before": before.reshape(P, -1),
    }


def build(nc, t, out):
    f32, f32r = mybir.dt.float32, mybir.dt.float32r
    ALU = mybir.AluOpType
    ACT = mybir.ActivationFunctionType
    AX = mybir.AxisListType
    add_sat = bass.dve_ops.TENSOR_ADD_SAT

    ctx = ExitStack()
    with ctx:
        def sb(name, shape, dt=f32, where=ctx):
            return where.enter_context(nc.sbuf_tensor(name, shape, dt))

        def sem(name, where=ctx):
            return where.enter_context(nc.semaphore(name))

        def scratch(name, shape, dt=f32):
            return nc.dram_tensor(name, shape, dt, kind="Internal").ap()

        xn_dram = scratch("xn_dram", (B, L, D))
        z_dram = scratch("z_dram", (B, P, KD, L))
        xs_dram = scratch("xs_dram", (2, B, L, D))
        bs_dram = scratch("bs_dram", (2, B, L, N_STATE))
        c_dram = scratch("c_dram", (B, N_STATE, L))

        def weight(name, shape):
            return sb(name + "_sb", shape)

        ident = weight("ident", [P, P])
        in_w = weight("in_w", [P, KD, 2 * D])
        in_b = weight("in_b", [P, 2 * KD])
        conv_w = weight("conv_w", [P, KD, TAPS])
        conv_b = weight("conv_b", [P, KD])
        b_w = weight("b_w", [P, KD, N_STATE])
        c_w = weight("c_w", [P, KD, N_STATE])
        c_b = weight("c_b", [N_STATE, 1])
        b_b = weight("b_b", [P, N_STATE])
        front = [("ident", ident), ("in_w", in_w), ("in_b", in_b), ("conv_w", conv_w), ("conv_b", conv_b),
                 ("b_w", b_w), ("c_w", c_w), ("c_b", c_b), ("b_b", b_b)]
        a_log = weight("a_log", [P, D])
        own_batch = weight("own_batch", [P, B])
        out_w = weight("out_w", [P, KD, D])
        rows = {n: weight(n, [P, D]) for n in
                ("out_b", "ln_w", "ln_b", "ln1_s", "ln1_b", "ln2_s", "ln2_b", "mlp_b2")}
        gate_w = weight("gate_w", [P, KD, E])
        gate_b = weight("gate_b", [P, E])
        before = weight("before", [P, E * E])
        f_w1 = weight("f_w1", [P, E, KD, F])
        f_b1 = weight("f_b1", [P, E, F // P])
        f_w2 = weight("f_w2", [P, E, F // P, D])
        f_b2 = weight("f_b2", [E, D])
        wq = weight("wq", [P, KD, GROUPS * P])
        wk = weight("wk", [P, KD, GROUPS * P])
        wv = weight("wv", [P, KD, D])
        wo = weight("wo", [P, KD, D])
        m_w1 = weight("m_w1", [P, KD, MLP])
        m_b1 = weight("m_b1", [P, MLP // P])
        m_w2 = weight("m_w2", [P, MLP // P, D])
        causal = weight("causal", [P, P])
        own_head = weight("own_head", [P, GROUPS * GH * HV])
        feature_eps = weight("feature_eps", [P, 1])
        back = [("a_log", a_log), ("own_batch", own_batch), ("out_w", out_w), *rows.items(),
                ("gate_w", gate_w), ("gate_b", gate_b), ("before", before), ("f_w1", f_w1), ("f_b1", f_b1),
                ("f_w2", f_w2), ("f_b2", f_b2), ("wq", wq), ("wk", wk), ("wv", wv), ("wo", wo),
                ("m_w1", m_w1), ("m_b1", m_b1), ("m_w2", m_w2), ("causal", causal), ("own_head", own_head),
                ("feature_eps", feature_eps)]

        bank = [ctx.enter_context(nc.psum_tensor(f"bank{i}", [P, 512], f32)) for i in range(8)]

        front_in = sem("front_in")
        back_in = sem("back_in")
        FRONT_IN, BACK_IN = 16 * len(front), 16 * len(back)

        front_part(nc, t, locals())
        main_part(nc, t, out, locals())


def front_part(nc, t, g):
    f32, f32r = mybir.dt.float32, mybir.dt.float32r
    ALU = mybir.AluOpType
    ACT = mybir.ActivationFunctionType
    bank, ident = g["bank"], g["ident"]
    in_w, in_b, conv_w, conv_b = g["in_w"], g["in_b"], g["conv_w"], g["conv_b"]
    b_w, b_b, c_w, c_b = g["b_w"], g["b_b"], g["c_w"], g["c_b"]
    front_in, FRONT_IN = g["front_in"], g["FRONT_IN"]
    NT = L // P
    LH = L // 2
    GR = NT // 2

    with ExitStack() as own:
        def sb(name, shape, dt=f32):
            return own.enter_context(nc.sbuf_tensor(name, shape, dt))

        def sem(name):
            return own.enter_context(nc.semaphore(name))

        xt = sb("xt", [P, NT, D])
        stats = sb("stats", [P, NT, 6])
        mv = sb("mv", [P, NT, 2])
        ve = sb("ve", [P, NT])
        rstd = sb("rstd", [P, NT])
        eps = sb("eps", [P, NT])
        mhalf = sb("mhalf", [P, NT])
        xnT = sb("xnT", [P, KD, L])
        xaT = sb("xaT", [P, KD, L + 3])
        zT = sb("zT", [P, KD, L])
        cv = sb("cv", [P, KD, L])
        xcT = sb("xcT", [P, KD, L])
        xhi = sb("xhi", [P, NT, D], f32r)
        xlo = sb("xlo", [P, NT, D], f32r)
        bt = sb("bt", [P, NT, N_STATE])
        bhi = sb("bhi", [P, NT, N_STATE], f32r)
        blo = sb("blo", [P, NT, N_STATE], f32r)
        cT = sb("cT", [N_STATE, L])

        x_in = sem("x_in")
        pads_set = sem("pads_set")
        stat_done = sem("stat_done")
        aggr_done = sem("aggr_done")
        ve_done = sem("ve_done")
        rstd_done = sem("rstd_done")
        ln_done = sem("ln_done")
        xn_out = sem("xn_out")
        tp_done = sem("tp_done")
        tp_copied = sem("tp_copied")
        proj_done = sem("proj_done")
        proj_read = sem("proj_read")
        z_out = sem("z_out")
        conv_step = sem("conv_step")
        conv_done = sem("conv_done")
        silu_done = sem("silu_done")
        back_done = sem("back_done")
        hi_done = sem("hi_done")
        lo_done = sem("lo_done")
        xs_out = sem("xs_out")
        bmm_done = sem("bmm_done")
        bt_done = sem("bt_done")
        bhi_done = sem("bhi_done")
        blo_done = sem("blo_done")
        bs_out = sem("bs_out")
        cmm_done = sem("cmm_done")
        cT_done = sem("cT_done")
        c_out = sem("c_out")
        NPROJ = 2 * 2 * KD
        PRIMED = 1
        primed = (xn_out, tp_done, silu_done, xs_out, bs_out, conv_done, z_out, back_done, cmm_done, c_out, lo_done, cT_done, bt_done)

        block = own.enter_context(nc.Block())

        @block.sync
        def _(sp):
            for n, tile in g["front"]:
                sp.dma_start(tile[:], t[n]).then_inc(front_in, 16)
            with sp.Fori(0, B) as b:
                sp.wait_ge(xn_out, PRIMED + 16 * b)
                sp.nop(nofuse=True)
                sp.wait_ge(tp_done, PRIMED + NT // 2 * b)
                sp.nop(nofuse=True)
                sp.dma_start(xt[:], t["x"][bass.ds(b, 1)].rearrange("b (i p) d -> p (b i) d", p=P)).then_inc(x_in, 16)
                sp.wait_ge(ln_done, NT * (b + 1))
                sp.nop(nofuse=True)
                sp.dma_start(g["xn_dram"][bass.ds(b, 1)].rearrange("b (i p) d -> p (b i) d", p=P), xt[:]).then_inc(xn_out, 16)
                sp.wait_ge(proj_read, NPROJ * (b + 1))
                sp.nop(nofuse=True)
                sp.dma_start(g["z_dram"][bass.ds(b, 1)].rearrange("b p k t -> p (b k) t"), zT[:]).then_inc(z_out, 16)
                sp.wait_ge(lo_done, PRIMED + NT * (b + 1))
                sp.nop(nofuse=True)
                sp.wait_ge(hi_done, NT * (b + 1))
                sp.nop(nofuse=True)
                for s, tile in enumerate((xhi, xlo)):
                    sp.dma_start(g["xs_dram"][s, bass.ds(b, 1)].rearrange("b (i p) d -> p (b i) d", p=P), tile[:].bitcast(f32)).then_inc(xs_out, 16)
                sp.wait_ge(blo_done, b + 1)
                sp.nop(nofuse=True)
                sp.wait_ge(bhi_done, b + 1)
                sp.nop(nofuse=True)
                for s, tile in enumerate((bhi, blo)):
                    sp.dma_start(g["bs_dram"][s, bass.ds(b, 1)].rearrange("b (i p) n -> p (b i) n", p=P), tile[:].bitcast(f32)).then_inc(bs_out, 16)
                sp.wait_ge(cT_done, PRIMED + 2 * (b + 1))
                sp.nop(nofuse=True)
                sp.dma_start(g["c_dram"][bass.ds(b, 1)].rearrange("b n t -> (b n) t"), cT[:]).then_inc(c_out, 16)
            for n, tile in g["back"]:
                sp.dma_start(tile[:], t[n]).then_inc(g["back_in"], 16)
            sp.wait_ge(xn_out, PRIMED + 16 * B)
            sp.wait_ge(z_out, PRIMED + 16 * B)
            sp.wait_ge(xs_out, PRIMED + 32 * B)
            sp.wait_ge(bs_out, PRIMED + 32 * B)
            sp.wait_ge(c_out, PRIMED + 16 * B)

        @block.vector
        def _(dve):
            dve.memset(xaT[:, :, 0:2], 0.0).then_inc(pads_set, 1)
            dve.memset(xaT[:, :, L + 2:L + 3], 0.0).then_inc(pads_set, 1)
            dve.wait_ge(front_in, FRONT_IN)
            with dve.Fori(0, B) as b:
                dve.wait_ge(x_in, 16 * (b + 1))
                for i in range(NT):
                    dve.bn_stats(stats[:, i, :], xt[:, i, :]).then_inc(stat_done, 1)
                dve.wait_ge(stat_done, NT * (b + 1))
                dve.nop(nofuse=True)
                for i in range(NT):
                    dve.bn_aggr(mv[:, i, :], stats[:, i, :]).then_inc(aggr_done, 1)
                dve.wait_ge(rstd_done, b + 1)
                for i in range(NT):
                    dve.tensor_scalar(xt[:, i, :], xt[:, i, :], mv[:, i, 0:1], rstd[:, i:i + 1],
                                      ALU.subtract, ALU.mult).then_inc(ln_done, 1)
                dve.wait_ge(proj_read, NPROJ * (b + 1))
                dve.wait_ge(pads_set, 2)
                dve.wait_ge(silu_done, PRIMED + KD * b)
                for k in range(KD):
                    dve.tensor_scalar(cv[:, k, :], xaT[:, k, 0:L], conv_w[:, k, 0:1], conv_b[:, k:k + 1],
                                      ALU.mult, ALU.add).then_inc(conv_step, 1)
                for j in range(1, TAPS):
                    for k in range(KD):
                        dve.wait_ge(conv_step, (TAPS - 1) * KD * b + KD * (j - 1) + k + 1)
                        step = dve.scalar_tensor_tensor(out=cv[:, k, :], in0=xaT[:, k, j:j + L], scalar=conv_w[:, k, j:j + 1],
                                                        in1=cv[:, k, :], op0=ALU.mult, op1=ALU.add)
                        step.then_inc(conv_step if j < TAPS - 1 else conv_done, 1)
                for i in range(NT):
                    if i == 0:
                        dve.wait_ge(xs_out, PRIMED + 32 * b)
                    dve.wait_ge(hi_done, NT * b + i + 1)
                    dve.tensor_tensor(xlo[:, i, :], bank[i % 4][:, 0:D], xhi[:, i, :].bitcast(f32), ALU.subtract).then_inc(lo_done, 1)
                dve.wait_ge(bmm_done, b + 1)
                dve.tensor_tensor(bt[:], bank[6][:, 0:NT * N_STATE].rearrange("p (i n) -> p i n", i=NT),
                                  b_b[:].unsqueeze(1).broadcast_to([P, NT, N_STATE]), ALU.add).then_inc(bt_done, 1)
                dve.wait_ge(bhi_done, b + 1)
                dve.wait_ge(bs_out, PRIMED + 32 * b)
                dve.tensor_tensor(blo[:], bt[:], bhi[:].bitcast(f32), ALU.subtract).then_inc(blo_done, 1)

        @block.gpsimd
        def _(pool):
            for s in primed:
                pool.sem_inc(s, PRIMED)
            pool.memset(eps[:], 1e-5).then_inc(pads_set, 1)
            pool.memset(mhalf[:], -0.5).then_inc(pads_set, 1)
            pool.wait_ge(pads_set, 4)
            with pool.Fori(0, B) as b:
                pool.wait_ge(aggr_done, NT * (b + 1))
                pool.tensor_tensor(ve[:], mv[:, :, 1], eps[:], ALU.add).then_inc(ve_done, 1)
                pool.wait_ge(ve_done, b + 1)
                pool.tensor_tensor(rstd[:], ve[:], mhalf[:], ALU.pow).then_inc(rstd_done, 1)

        @block.scalar
        def _(act):
            act.wait_ge(front_in, FRONT_IN)
            with act.Fori(0, B) as b:
                for i in range(NT // 2):
                    act.wait_ge(tp_done, PRIMED + NT // 2 * b + i + 1)
                    act.activation(xnT[:, :, 2 * P * i:2 * P * (i + 1)].rearrange("p k (i q) -> p k i q", i=2),
                                   bank[i % 2][:].rearrange("p (i k q) -> p k i q", i=2, k=KD), ACT.Copy).then_inc(tp_copied, 1)
                for h in range(2):
                    for m in range(2 * KD):
                        n = 2 * KD * h + m
                        act.wait_ge(proj_done, NPROJ * b + n + 1)
                        if n == 0:
                            act.wait_ge(conv_done, PRIMED + KD * b)
                            act.wait_ge(z_out, PRIMED + 16 * b)
                        src = bank[2 + n % 4][:]
                        if m < KD:
                            act.activation(xaT[:, m, 2 + LH * h:2 + LH * (h + 1)], src, ACT.Identity,
                                           bias=in_b[:, m:m + 1]).then_inc(proj_read, 1)
                        else:
                            act.activation(zT[:, m - KD, LH * h:LH * (h + 1)], src, ACT.Silu,
                                           bias=in_b[:, m:m + 1]).then_inc(proj_read, 1)
                act.wait_ge(back_done, PRIMED + NT * b)
                act.wait_ge(cmm_done, PRIMED + 2 * b)
                for k in range(KD):
                    act.wait_ge(conv_done, PRIMED + KD * b + k + 1)
                    act.activation(xcT[:, k, :], cv[:, k, :], ACT.Silu).then_inc(silu_done, 1)
                act.wait_ge(xs_out, PRIMED + 32 * b)
                for i in range(NT):
                    act.wait_ge(back_done, PRIMED + NT * b + i + 1)
                    act.activation(xhi[:, i, :], bank[i % 4][:, 0:D], ACT.Copy).then_inc(hi_done, 1)
                act.wait_ge(bs_out, PRIMED + 32 * b)
                act.wait_ge(bt_done, PRIMED + b + 1)
                act.activation(bhi[:], bt[:], ACT.Copy).then_inc(bhi_done, 1)
                act.wait_ge(c_out, PRIMED + 16 * b)
                for h in range(2):
                    act.wait_ge(cmm_done, PRIMED + 2 * b + h + 1)
                    act.activation(cT[:, LH * h:LH * (h + 1)], bank[4 + h][0:N_STATE, :], ACT.Identity,
                                   bias=c_b[:, 0:1]).then_inc(cT_done, 1)

        @block.tensor
        def _(pe):
            pe.wait_ge(front_in, FRONT_IN)
            with pe.Fori(0, B) as b:
                pe.wait_ge(lo_done, PRIMED + NT * b)
                for i in range(NT // 2):
                    for j in range(2):
                        pe.wait_ge(ln_done, NT * b + 2 * i + j + 1)
                        if i >= 2:
                            pe.wait_ge(tp_copied, NT // 2 * b + i - 1)
                        for k in range(KD):
                            last = pe.transpose(bank[i % 2][:, (KD * j + k) * P:(KD * j + k + 1) * P],
                                                xt[:, 2 * i + j, k * P:(k + 1) * P], ident[:])
                    last.then_inc(tp_done, 1)
                for h in range(2):
                    pe.wait_ge(tp_copied, NT // 2 * b + NT // 4 * (h + 1))
                    for m in range(2 * KD):
                        n = 2 * KD * h + m
                        if n == 0:
                            pe.wait_ge(cT_done, PRIMED + 2 * b)
                        if n >= 4:
                            pe.wait_ge(proj_read, NPROJ * b + n - 3)
                        for k in range(KD):
                            last = pe.matmul(bank[2 + n % 4][:], in_w[:, k, m * P:(m + 1) * P],
                                             xnT[:, k, LH * h:LH * (h + 1)], start=(k == 0), stop=(k == KD - 1))
                        last.then_inc(proj_done, 1)
                pe.wait_ge(silu_done, PRIMED + KD * (b + 1))
                pe.wait_ge(tp_copied, NT // 2 * (b + 1))
                pe.wait_ge(proj_read, NPROJ * (b + 1))
                for i in range(NT):
                    if i >= 4:
                        pe.wait_ge(lo_done, PRIMED + NT * b + i - 3)
                    for k in range(KD):
                        last = pe.transpose(bank[i % 4][:, k * P:(k + 1) * P], xcT[:, k, i * P:(i + 1) * P], ident[:])
                    last.then_inc(back_done, 1)
                pe.wait_ge(bt_done, PRIMED + b)
                for i in range(NT):
                    for k in range(KD):
                        last = pe.matmul(bank[6][:, i * N_STATE:(i + 1) * N_STATE], xcT[:, k, i * P:(i + 1) * P],
                                         b_w[:, k, :], start=(k == 0), stop=(k == KD - 1))
                last.then_inc(bmm_done, 1)
                for h in range(2):
                    for k in range(KD):
                        last = pe.matmul(bank[4 + h][0:N_STATE, :], c_w[:, k, :], xcT[:, k, LH * h:LH * (h + 1)],
                                         start=(k == 0), stop=(k == KD - 1))
                    last.then_inc(cmm_done, 1)


class Signal:

    def __init__(self, sem, per_chunk, before=0):
        self.sem, self.per_chunk, self.before = sem, per_chunk, before

    def after(self, chunk, n):
        return chunk * self.per_chunk + (n + self.before)


def main_part(nc, t, out, g):
    f32, f32r = mybir.dt.float32, mybir.dt.float32r
    ALU = mybir.AluOpType
    ACT = mybir.ActivationFunctionType
    AX = mybir.AxisListType
    add_sat = g["add_sat"]
    bank, ident, rows = g["bank"], g["ident"], g["rows"]
    BACK_IN = g["BACK_IN"]
    LNS = 6
    MAMBA, FFN1, OUTER, LN1, LN2, FFN2 = range(LNS)
    LN_EPS = {MAMBA: 1e-5, FFN1: 1e-5, OUTER: 1e-5, LN1: 1e-6, LN2: 1e-6, FFN2: 1e-5}
    TPOSES = 5
    T_FFN1, T_ATT, T_WO, T_MLP, T_FFN2 = range(TPOSES)

    with ExitStack() as own:
        def sb(name, shape, dt=f32):
            return own.enter_context(nc.sbuf_tensor(name, shape, dt))

        def signal(name, per_chunk, before=0):
            return Signal(own.enter_context(nc.semaphore(name)), per_chunk, before)

        def signals(name, count, per_chunk, before=0):
            return [signal(f"{name}{k}", per_chunk, before) for k in range(count)]

        decay = sb("decay", [P, D])
        xrows = sb("xrows", [P, QT, D], f32r)
        brows = sb("brows", [P, QT, B, N_STATE], f32r)
        cT = sb("cT_all", [P, L + CT])
        cblk = sb("cblk", [P, CT * YROWS + YROWS])
        decayed_state = sb("decayed_state", [P, D])
        state = sb("state", [P, RING, D])
        x_t = sb("x_t", [P, TILES, D])
        xn_t = sb("xn_t", [P, TILES, D])
        z_t = sb("z_t", [P, KD, B, CT])
        xnb = sb("xnb", [P, TILES, D])
        xb = sb("xb", [P, TILES, D])
        gT = sb("gT", [P, KD, B, CT])
        h_t = sb("h_t", [P, TILES, D])
        turn = sb("turn", [P, TILES, D])
        x1 = sb("x1", [P, TILES, D])
        acc = sb("acc", [P, TILES, D])
        a_t = sb("a_t", [P, TILES, D])
        xr = sb("xr", [P, TILES, D])
        mb = sb("mb", [P, TILES, D])
        x3 = sb("x3", [P, TILES, D])
        stats = sb("m_stats", [P, TILES, 6])
        mv = sb("m_mv", [P, LNS, TILES, 2])
        ve = sb("m_ve", [P, LNS, TILES])
        rstd = sb("m_rstd", [P, LNS, TILES])
        eps = sb("m_eps", [P, LNS, TILES])
        mhalf = sb("m_mhalf", [P, TILES])
        late_turn = sb("late_turn", [P, TILES, D])
        fT = sb("fT", [P, KD, TOK])
        late_fT = sb("late_fT", [P, KD, TOK])
        score = sb("score", [P, TILES, E])
        above = sb("above", [P, TILES, E * E])
        level = sb("level", [P, TILES, E * E])
        rank = sb("rank", [P, TILES, E])
        comb = sb("comb", [P, 2, TILES, E])
        combT = sb("combT", [E, TOK])
        hs = sb("hs", [P, 2, F // P, TOK])
        kT = sb("kT", [P, GROUPS, TOK])
        qT = sb("qT", [P, GROUPS, TOK])
        ktok = sb("ktok", [P, TILES, GROUPS * P])
        vv = sb("vv", [P, TILES, H, HV])
        ss = sb("ss", [P, GH, GROUPS, P])
        kv = sb("kv", [P, B, GROUPS * GH * HV])
        kvm = sb("kvm", [P, B, GROUPS * GH * HV])
        rec = sb("rec", [P, TILES, H])
        mh = sb("mh", [P, MLP // P, TOK])

        U, Y, HB, OB, TB = [bank[0], bank[1]], bank[2], [bank[3], bank[4]], [bank[5], bank[6]], bank[7]

        ROW_DMAS = 2 + B * 2
        rows_in = [signal(f"rows_in{q}", 16 * ROW_DMAS) for q in range(QUARTERS)]
        c_in = signal("c_in", 0)
        tok_in = signal("tok_in", 16 * 3 * B)
        stored = signal("stored", 16 * B, before=1)
        set_up = signal("set_up", 0)
        decayed = signal("decayed", 2 * CT)
        stepped = signal("stepped", 2 * CT, before=2)
        cblk_set = signal("cblk_set", 2 * QUARTERS)
        y_gated = signal("y_gated", 1)
        h_done = signal("h_done", 1, before=1)
        bn_done = signals("bn_done", LNS, TILES)
        aggr_done = signals("aggr_done", LNS, TILES)
        u_done = signals("u_done", LNS, TILES)
        x1_done = signal("x1_done", TILES, before=1)
        xf_done = signals("xf_done", 2, TILES)
        route = signals("route", 2, 1 + TILES * 6)
        comb_done = signals("comb_done", 2, TILES)
        acc_set = signals("acc_set", 2, 1)
        acc_done = signals("acc_done", 2, E * TILES, before=1)
        a_done = signal("a_done", TILES)
        xl_done = signal("xl_done", TILES)
        kT_done = signal("kT_done", 2)
        qT_done = signal("qT_done", 2)
        masked = signal("masked", TILES * GH)
        kv_masked = signal("kv_masked", B)
        rec_done = signal("rec_done", TILES)
        at_done = signal("at_done", TILES)
        xr_done = signal("xr_done", 1)
        yl_done = signal("yl_done", TILES)
        x3_done = signal("x3_done", 1)
        u_made = signal("u_made", PAIRS)
        y_made = signal("y_made", PAIRS)
        y_tposed = signal("y_tposed", 1)
        mamba_out = signal("mamba_out", 1)
        tposed = signals("tposed", TPOSES, 1)
        gated = signals("gated", 2, 1)
        comb_tposed = signals("comb_tposed", 2, 1)
        bias_made = signals("bias_made", 2, 1)
        hidden = signals("hidden", 2, E)
        expert_out = signals("expert_out", 2, E)
        k_made = signal("k_made", 2)
        q_made = signal("q_made", 2)
        v_made = signal("v_made", 1)
        k_tposed = signal("k_tposed", TILES)
        scored = signal("scored", TILES * GH)
        num_made = signal("num_made", TILES)
        kv_made = signal("kv_made", B)
        wo_made = signal("wo_made", 1)
        mlp_hidden = signal("mlp_hidden", 4)
        mlp_made = signal("mlp_made", 1)
        exp_done = signal("exp_done", 0)
        y_copied = signal("y_copied", 1, before=1)
        tcopied = signals("tcopied", TPOSES, 1)
        comb_copied = signals("comb_copied", 2, 1)
        relued = signals("relued", 2, E * (F // P))
        v_copied = signal("v_copied", TILES)
        k_copied = signal("k_copied", TILES)
        gelued = signal("gelued", MLP // P)
        pool_set = signal("pool_set", 0)
        xnb_done = signal("xnb_done", 1)
        xb_done = signal("xb_done", 1)
        ve_done = signals("ve_done", LNS, 1)
        rstd_done = signals("rstd_done", LNS, 1)
        kv_added = signal("kv_added", B, before=1)
        mb_done = signal("mb_done", 2)
        primed = (h_done, x1_done, *acc_done, y_copied, kv_added, stored)
        POOL_SETS = 9 + LNS
        COMB_AFTER = 3

        block = own.enter_context(nc.Block())

        def load_rows(sp, chunk, q):
            t0 = chunk * CT + q * QT
            for j in range(2):
                sp.dma_start(xrows[32 * q + 2 * B * j:32 * q + 2 * B * (j + 1)].bitcast(f32),
                             g["xs_dram"][:, :, bass.ds(t0, QT), :].rearrange("s b t d -> (s b) t d")).then_inc(rows_in[q].sem, 16)
            for b in range(B):
                for s in range(2):
                    at0 = 32 * q + 2 * B * s + b
                    sp.dma_start(brows[at0:at0 + B + 1:B, :, b, :].bitcast(f32),
                                 g["bs_dram"][s:s + 1, b, bass.ds(t0, QT), :].broadcast_to([2, QT, N_STATE])).then_inc(rows_in[q].sem, 16)

        def load_tokens(sp, chunk):
            for b in range(B):
                p0 = (b % 2) * CT
                rows_of = (slice(p0, p0 + CT), b // 2)
                sp.dma_start(x_t[rows_of], t["x"][b, bass.ds(chunk * CT, CT), :]).then_inc(tok_in.sem, 16)
                sp.dma_start(xn_t[rows_of], g["xn_dram"][b, bass.ds(chunk * CT, CT), :]).then_inc(tok_in.sem, 16)
                sp.dma_start(z_t[:, :, b, :], g["z_dram"][b, :, :, bass.ds(chunk * CT, CT)]).then_inc(tok_in.sem, 16)

        @block.sync
        def _(sp):
            sp.dma_start(cT[:, 0:L], g["c_dram"].rearrange("b n t -> (b n) t")).then_inc(c_in.sem, 16)
            sp.wait_ge(pool_set.sem, POOL_SETS)
            for q in range(QUARTERS):
                load_rows(sp, 0, q)
            sp.wait_ge(g["back_in"], BACK_IN)

            def wait_apart(signal_, value):
                sp.wait_ge(signal_.sem, value)
                sp.nop(nofuse=True)

            def chunk_loads(i, more):
                load_tokens(sp, i)
                if more:
                    for q in range(QUARTERS):
                        wait_apart(u_made, u_made.after(i, PAIRS // QUARTERS * (q + 1)))
                        load_rows(sp, i + 1, q)

            def store(c):
                for b in range(B):
                    p0 = (b % 2) * CT
                    sp.dma_start(out[b, bass.ds(c * CT, CT), :], x3[p0:p0 + CT, b // 2]).then_inc(stored.sem, 16)

            def tokens_free(c):
                wait_apart(y_gated, y_gated.after(c, 1))
                wait_apart(xnb_done, xnb_done.after(c, 1))
                wait_apart(xb_done, xb_done.after(c, 1))

            def finish(c):
                wait_apart(acc_done[1], acc_done[1].after(c, E * TILES))
                store(c)

            chunk_loads(0, True)
            tokens_free(0)
            chunk_loads(1, True)
            with sp.Fori(2, CHUNKS - 1) as i:
                tokens_free(i - 1)
                chunk_loads(i, True)
                finish(i - 2)
            tokens_free(CHUNKS - 2)
            chunk_loads(CHUNKS - 1, False)
            for c in range(CHUNKS - 3, CHUNKS):
                finish(c)
            sp.wait_ge(stored.sem, stored.after(CHUNKS - 1, 16 * B))

        @block.gpsimd
        def _(pool):
            for s in primed:
                pool.sem_inc(s.sem, 1)
            pool.memset(brows[:].bitcast(f32), 0.0).then_inc(pool_set.sem, 1)
            pool.memset(cblk[:], 0.0).then_inc(pool_set.sem, 1)
            pool.memset(cT[:, L:L + CT], 0.0).then_inc(pool_set.sem, 1)
            pool.memset(mhalf[:], -0.5).then_inc(pool_set.sem, 1)
            for k, value in LN_EPS.items():
                pool.memset(eps[:, k], value).then_inc(pool_set.sem, 1)
            pool.memset(kv[:], 0.0).then_inc(pool_set.sem, 1)
            pool.memset(vv[:], 1.0).then_inc(pool_set.sem, 1)
            pool.memset(state[:, RING - 1], 0.0).then_inc(pool_set.sem, 1)
            pool.memset(ve[:], 0.0).then_inc(pool_set.sem, 1)
            pool.memset(rstd[:], 0.0).then_inc(pool_set.sem, 1)
            pool.wait_ge(pool_set.sem, POOL_SETS)
            pool.wait_ge(g["back_in"], BACK_IN)

            def rstd_of(c, k):
                pool.wait_ge(aggr_done[k].sem, aggr_done[k].after(c, TILES))
                pool.tensor_tensor(ve[:, k], mv[:, k, :, 1], eps[:, k], ALU.add).then_inc(ve_done[k].sem, 1)
                pool.wait_ge(ve_done[k].sem, ve_done[k].after(c, 1))
                pool.tensor_tensor(rstd[:, k], ve[:, k], mhalf[:], ALU.pow).then_inc(rstd_done[k].sem, 1)

            def both(row):
                return rows[row][:].unsqueeze(1).broadcast_to([P, TILES, D])

            def step(c, late):
                if c is None:
                    rstd_of(late, FFN2)
                    return
                pool.wait_ge(tok_in.sem, tok_in.after(c, 16 * 3 * B))
                pool.wait_ge(h_done.sem, h_done.after(c, 0))
                pool.tensor_tensor(xnb[:], xn_t[:], both("out_b"), ALU.add).then_inc(xnb_done.sem, 1)
                pool.wait_ge(x1_done.sem, x1_done.after(c, 0))
                pool.tensor_tensor(xb[:], x_t[:], both("ln_b"), ALU.add).then_inc(xb_done.sem, 1)
                rstd_of(c, MAMBA)
                rstd_of(c, FFN1)
                if late is not None:
                    rstd_of(late, FFN2)
                rstd_of(c, OUTER)
                if late is not None:
                    pool.wait_ge(x3_done.sem, x3_done.after(late, 1))
                pool.tensor_tensor(mb[:], acc[:], both("mlp_b2"), ALU.add).then_inc(mb_done.sem, 1)
                rstd_of(c, LN1)
                for b in range(B):
                    pool.wait_ge(kv_masked.sem, kv_masked.after(c, b + 1))
                    pool.tensor_tensor(kv[:, b], kv[:, b], kvm[:, b], ALU.add).then_inc(kv_added.sem, 1)
                pool.wait_ge(xr_done.sem, xr_done.after(c, 1))
                pool.wait_ge(mb_done.sem, mb_done.after(c, 1))
                pool.tensor_tensor(mb[:], mb[:], xr[:], ALU.add).then_inc(mb_done.sem, 1)
                rstd_of(c, LN2)

            step(0, None)
            with pool.Fori(2, CHUNKS) as i:
                step(i - 1, i - 2)
            step(CHUNKS - 1, CHUNKS - 2)
            step(None, CHUNKS - 1)

        @block.scalar
        def _(act):
            act.wait_ge(set_up.sem, 1)
            act.activation(decay[:], decay[:], ACT.Exp).then_inc(exp_done.sem, 1)
            act.wait_ge(g["back_in"], BACK_IN)
            act.wait_ge(pool_set.sem, POOL_SETS)

            def copy_set(c, k):
                act.wait_ge(tposed[k].sem, tposed[k].after(c, 1))
                dst = late_fT if k in (T_MLP, T_FFN2) else fT
                act.activation(dst[:].rearrange("p k q -> p (k q)"), TB[:], ACT.Copy).then_inc(tcopied[k].sem, 1)

            def relu(c, f, e):
                act.wait_ge(hidden[f].sem, hidden[f].after(c, e + 1))
                for m in range(F // P):
                    act.activation(hs[:, e % 2, m], HB[e % 2][:, m * TOK:(m + 1) * TOK], ACT.Relu,
                                   bias=g["f_b1"][:, e, m:m + 1]).then_inc(relued[f].sem, 1)

            def copy_comb(c, f):
                act.wait_ge(comb_tposed[f].sem, comb_tposed[f].after(c, 1))
                act.activation(combT[:], TB[0:E, 0:TOK], ACT.Copy).then_inc(comb_copied[f].sem, 1)

            def gelu(late, j):
                if late is None:
                    return
                act.wait_ge(mlp_hidden.sem, mlp_hidden.after(late, j + 1))
                for m in (2 * j, 2 * j + 1):
                    act.activation(mh[:, m], HB[j % 2][:, m % 2 * TOK:(m % 2 + 1) * TOK], ACT.Gelu_apprx_tanh,
                                   bias=g["m_b1"][:, m:m + 1]).then_inc(gelued.sem, 1)

            def step(c, late):
                if late is not None:
                    copy_set(late, T_MLP)
                if c is not None:
                    act.wait_ge(y_made.sem, y_made.after(c, PAIRS))
                    act.activation(turn[:].rearrange("p i d -> p (i d)"), Y[:], ACT.Copy).then_inc(y_copied.sem, 1)
                for j in range(4):
                    gelu(late, j)
                if c is not None:
                    copy_set(c, T_FFN1)
                    relu(c, 0, 0)
                    relu(c, 0, 1)
                    copy_comb(c, 0)
                if late is not None:
                    copy_set(late, T_FFN2)
                if c is not None:
                    for e in range(2, E):
                        relu(c, 0, e)
                        if e == COMB_AFTER + 1 and late is not None:
                            copy_comb(late, 1)
                if late is not None:
                    if c is None:
                        copy_comb(late, 1)
                    for e in range(4):
                        relu(late, 1, e)
                if c is not None:
                    copy_set(c, T_ATT)
                    act.wait_ge(v_made.sem, v_made.after(c, 1))
                    for n in range(TILES):
                        act.activation(vv[:, n, :, 0:DH], TB[:, n * D:(n + 1) * D].rearrange("p (h m) -> p h m", h=H),
                                       ACT.Copy).then_inc(v_copied.sem, 1)
                    for n in range(TILES):
                        act.wait_ge(k_tposed.sem, k_tposed.after(c, n + 1))
                        act.activation(ktok[:, n], OB[n][:], ACT.Copy).then_inc(k_copied.sem, 1)
                if late is not None:
                    relu(late, 1, 4)
                    relu(late, 1, 5)
                if c is not None:
                    copy_set(c, T_WO)
                if late is not None:
                    relu(late, 1, 6)
                    relu(late, 1, 7)

            step(0, None)
            with act.Fori(2, CHUNKS) as i:
                step(i - 1, i - 2)
            step(CHUNKS - 1, CHUNKS - 2)
            step(None, CHUNKS - 1)

        @block.tensor
        def _(pe):
            pe.wait_ge(g["back_in"], BACK_IN)
            pe.wait_ge(pool_set.sem, POOL_SETS)
            pe.wait_ge(exp_done.sem, 1)

            def scan_inputs(i, n):
                q, first = divmod(n, PAIRS // QUARTERS)
                if first == 0:
                    pe.wait_ge(rows_in[q].sem, rows_in[q].after(i, 16 * ROW_DMAS))
                if not (isinstance(i, int) and i == 0 and n < 2):
                    pe.wait_ge(stepped.sem, stepped.after(i, 4 * (n - 1)))
                for j in range(2):
                    tq = (2 * n + j) % QT
                    last = pe.matmul(U[n % 2][:, j * D:(j + 1) * D], brows[32 * q:32 * q + ROWS, tq].rearrange("r b n -> r (b n)"),
                                     xrows[32 * q:32 * q + ROWS, tq, :], start=True, stop=True)
                last.then_inc(u_made.sem, 1)

            def scan_output(i, n):
                if n == 0:
                    pe.wait_ge(y_copied.sem, y_copied.after(i, 0))
                if n % (PAIRS // QUARTERS) == 0:
                    pe.wait_ge(cblk_set.sem, cblk_set.after(i, 2 * (n // (PAIRS // QUARTERS) + 1)))
                pe.wait_ge(stepped.sem, stepped.after(i, 4 * (n + 1)))
                for s in (2 * n, 2 * n + 1):
                    tile, row = divmod(s // YSTEPS * YROWS, P)
                    last = pe.matmul(Y[row:row + YROWS, tile * D:(tile + 1) * D], cblk[:, s * YROWS:(s + 1) * YROWS],
                                     state[:, s % RING, :], start=(s % YSTEPS == 0), stop=(s % YSTEPS == YSTEPS - 1),
                                     tile_position=(0, row))
                last.then_inc(y_made.sem, 1)

            def step(i, c, late):
                at_pair = [0]

                def scan(pairs):
                    for _ in range(pairs if i is not None else 0):
                        n = at_pair[0]
                        if n + 1 < PAIRS:
                            scan_inputs(i, n + 1)
                        if n >= 2:
                            scan_output(i, n - 2)
                        at_pair[0] += 1

                def transposes(src):
                    for tile in range(TILES):
                        for kk in range(KD):
                            last = pe.transpose(TB[:, kk * TOK + tile * P:kk * TOK + (tile + 1) * P],
                                                src[:, tile, kk * P:(kk + 1) * P], ident[:])
                    return last

                def tpose_set(c, k, done):
                    pe.wait_ge(done.sem, done.after(c, TILES))
                    transposes(late_turn if k in (T_MLP, T_FFN2) else turn).then_inc(tposed[k].sem, 1)

                def gate(c, f):
                    k_set, src = ((T_FFN1, fT), (T_FFN2, late_fT))[f]
                    pe.wait_ge(tcopied[k_set].sem, tcopied[k_set].after(c, 1))
                    for tile in range(TILES):
                        for k in range(KD):
                            last = pe.matmul(TB[:, tile * E:(tile + 1) * E], src[:, k, tile * P:(tile + 1) * P],
                                             g["gate_w"][:, k, :], start=(k == 0), stop=(k == KD - 1))
                    last.then_inc(gated[f].sem, 1)

                def turn_comb(c, f):
                    pe.wait_ge(comb_done[f].sem, comb_done[f].after(c, TILES))
                    for tile in range(TILES):
                        last = pe.transpose(TB[0:E, tile * P:(tile + 1) * P], comb[:, f, tile, :], ident[:])
                    last.then_inc(comb_tposed[f].sem, 1)

                def bias(c, f):
                    pe.wait_ge(comb_copied[f].sem, comb_copied[f].after(c, 1))
                    for tile in range(TILES):
                        last = pe.matmul(TB[:, tile * D:(tile + 1) * D], combT[:, tile * P:(tile + 1) * P],
                                         g["f_b2"][:], start=True, stop=True)
                    last.then_inc(bias_made[f].sem, 1)

                def first_layer(c, f, e):
                    src = (fT, late_fT)[f]
                    if e >= 2:
                        pe.wait_ge(relued[f].sem, relued[f].after(c, F // P * (e - 1)))
                    for m in range(F // P):
                        for k in range(KD):
                            last = pe.matmul(HB[e % 2][:, m * TOK:(m + 1) * TOK], g["f_w1"][:, e, k, m * P:(m + 1) * P],
                                             src[:, k, :], start=(k == 0), stop=(k == KD - 1))
                    last.then_inc(hidden[f].sem, 1)

                def second_layer(c, f, e):
                    pe.wait_ge(relued[f].sem, relued[f].after(c, F // P * (e + 1)))
                    if e >= 2:
                        pe.wait_ge(acc_done[f].sem, acc_done[f].after(c, TILES * (e - 1)))
                    for tile in range(TILES):
                        for m in range(F // P):
                            last = pe.matmul(OB[(e + 1) % 2][:, tile * D:(tile + 1) * D],
                                             hs[:, e % 2, m, tile * P:(tile + 1) * P], g["f_w2"][:, e, m, :],
                                             start=(m == 0), stop=(m == F // P - 1))
                    last.then_inc(expert_out[f].sem, 1)

                def mlp_input(c):
                    tpose_set(c, T_MLP, yl_done)
                    pe.wait_ge(tcopied[T_MLP].sem, tcopied[T_MLP].after(c, 1))

                def mlp_first(c, j):
                    if c is None:
                        return
                    if j >= 2:
                        pe.wait_ge(gelued.sem, gelued.after(c, 2 * (j - 1)))
                    for m in (2 * j, 2 * j + 1):
                        for k in range(KD):
                            last = pe.matmul(HB[j % 2][:, m % 2 * TOK:(m % 2 + 1) * TOK], g["m_w1"][:, k, m * P:(m + 1) * P],
                                             late_fT[:, k, :], start=(k == 0), stop=(k == KD - 1))
                    last.then_inc(mlp_hidden.sem, 1)

                def late_experts(first, end, scans):
                    first_layer(late, 1, first)
                    if first + 1 < end:
                        first_layer(late, 1, first + 1)
                    for e in range(first, end):
                        if first < e < end - 1:
                            first_layer(late, 1, e + 1)
                        scan(scans)
                        if c is not None and e == 0:
                            pe.wait_ge(acc_done[0].sem, acc_done[0].after(c, TILES * (E - 1)))
                        elif c is not None and e == 1:
                            pe.wait_ge(acc_done[0].sem, acc_done[0].after(c, TILES * E))
                        second_layer(late, 1, e)

                if i is not None:
                    scan_inputs(i, 0)
                scan(1)
                mlp_first(late, 1)
                if late is not None:
                    pe.wait_ge(acc_done[1].sem, acc_done[1].after(late, 0))
                if c is not None:
                    pe.wait_ge(y_copied.sem, y_copied.after(c, 1))
                    transposes(turn).then_inc(y_tposed.sem, 1)
                scan(1)
                mlp_first(late, 2)
                scan(1)
                if c is not None:
                    pe.wait_ge(y_gated.sem, y_gated.after(c, 1))
                    for tile in range(TILES):
                        for k in range(KD):
                            last = pe.matmul(OB[0][:, tile * D:(tile + 1) * D],
                                             gT[:, k, 2 * tile:2 * tile + 2, :], g["out_w"][:, k, :],
                                             start=(k == 0), stop=(k == KD - 1))
                    last.then_inc(mamba_out.sem, 1)
                mlp_first(late, 3)
                for m in range(MLP // P):
                    if late is not None:
                        pe.wait_ge(gelued.sem, gelued.after(late, m + 1))
                        for tile in range(TILES):
                            last = pe.matmul(OB[1][:, tile * D:(tile + 1) * D], mh[:, m, tile * P:(tile + 1) * P],
                                             g["m_w2"][:, m, :], start=(m == 0 and tile == 0), stop=(m == MLP // P - 1),
                                             skip_group_check=True)
                    if m % 3 == 2:
                        scan(1)
                scan(1)
                if late is not None:
                    last.then_inc(mlp_made.sem, 1)
                if c is not None:
                    tpose_set(c, T_FFN1, xf_done[0])
                    gate(c, 0)
                    first_layer(c, 0, 0)
                    first_layer(c, 0, 1)
                scan(1)
                if c is not None:
                    turn_comb(c, 0)
                    bias(c, 0)
                    pe.wait_ge(acc_set[0].sem, acc_set[0].after(c, 1))
                if late is not None:
                    tpose_set(late, T_FFN2, xf_done[1])
                for e in range(E):
                    if c is not None:
                        if 1 <= e < E - 1:
                            first_layer(c, 0, e + 1)
                        scan(1)
                        second_layer(c, 0, e)
                    else:
                        scan(1)
                    if late is not None:
                        if e == 0:
                            gate(late, 1)
                        if e == COMB_AFTER:
                            turn_comb(late, 1)
                        if e == COMB_AFTER + 1:
                            bias(late, 1)
                if late is not None:
                    late_experts(0, 4, 1)
                    pe.wait_ge(acc_set[1].sem, acc_set[1].after(late, 1))
                if c is None:
                    if late is not None:
                        late_experts(4, 6, 1)
                        late_experts(6, 8, 1)
                        return
                    scan(PAIRS - at_pair[0])
                    scan_output(i, PAIRS - 2)
                    scan_output(i, PAIRS - 1)
                    return
                tpose_set(c, T_ATT, xl_done)
                pe.wait_ge(tcopied[T_ATT].sem, tcopied[T_ATT].after(c, 1))
                if late is not None:
                    pe.wait_ge(acc_done[1].sem, acc_done[1].after(late, TILES * 4))
                for w, bs, made in ((g["wk"], HB, k_made), (g["wq"], OB, q_made)):
                    for gr in range(GROUPS):
                        for k in range(KD):
                            last = pe.matmul(bs[gr // 2][:, gr % 2 * TOK:(gr % 2 + 1) * TOK], w[:, k, gr * P:(gr + 1) * P],
                                             fT[:, k, :], start=(k == 0), stop=(k == KD - 1))
                        if gr % 2:
                            last.then_inc(made.sem, 1)
                    if made is k_made:
                        scan(1)
                for tile in range(TILES):
                    for k in range(KD):
                        last = pe.matmul(TB[:, tile * D:(tile + 1) * D], fT[:, k, tile * P:(tile + 1) * P],
                                         g["wv"][:, k, :], start=(k == 0), stop=(k == KD - 1))
                last.then_inc(v_made.sem, 1)
                scan(1)
                pe.wait_ge(kT_done.sem, kT_done.after(c, 2))
                pe.wait_ge(qT_done.sem, qT_done.after(c, 2))
                for tile in range(TILES):
                    for gr in range(GROUPS):
                        last = pe.transpose(OB[tile][:, gr * P:(gr + 1) * P], kT[:, gr, tile * P:(tile + 1) * P], ident[:])
                    last.then_inc(k_tposed.sem, 1)
                pe.wait_ge(v_copied.sem, v_copied.after(c, TILES))
                pe.wait_ge(k_copied.sem, k_copied.after(c, TILES))
                pe.wait_ge(kv_added.sem, kv_added.after(c, 0))
                for tile in range(TILES):
                    SB = (HB[0], HB[1], TB, OB[1])
                    tok = slice(tile * P, (tile + 1) * P)
                    for hh in range(GH):
                        if tile:
                            pe.wait_ge(masked.sem, masked.after(c, GH * (tile - 1) + hh + 1))
                        for gr in range(GROUPS):
                            last = pe.matmul(SB[hh][:, gr * P:(gr + 1) * P], kT[PADH * hh:PADH * (hh + 1), gr, tok],
                                             qT[PADH * hh:PADH * (hh + 1), gr, tok], start=True, stop=True)
                        last.then_inc(scored.sem, 1)
                    if tile:
                        pe.wait_ge(at_done.sem, at_done.after(c, tile))
                    W = GH * HV
                    for bb in range(2):
                        b = 2 * tile + bb
                        for gr in range(GROUPS):
                            pe.matmul(OB[0][CT * bb:CT * (bb + 1), gr * W:(gr + 1) * W],
                                      qT[:, gr, tile * P + CT * bb:tile * P + CT * (bb + 1)],
                                      kv[:, b, gr * W:(gr + 1) * W], start=(gr == 0), stop=False, skip_group_check=True)
                    scan(1)
                    for hh in range(GH):
                        pe.wait_ge(masked.sem, masked.after(c, GH * tile + hh + 1))
                        for gr in range(GROUPS):
                            hd = gr * GH + hh
                            last = pe.matmul(OB[0][:, hd * HV:(hd + 1) * HV], ss[:, hh, gr, :], vv[:, tile, hd, :],
                                             start=False, stop=(hh == GH - 1), skip_group_check=True)
                        if hh == 1:
                            scan(1)
                    last.then_inc(num_made.sem, 1)
                for b in range(B):
                    if b >= 2:
                        pe.wait_ge(kv_masked.sem, kv_masked.after(c, b - 1))
                    part = slice(CT * (b % 2), CT * (b % 2 + 1))
                    for gr in range(GROUPS):
                        last = pe.matmul(HB[b % 2][:, gr * W:(gr + 1) * W], ktok[part, b // 2, gr * P:(gr + 1) * P],
                                         vv[part, b // 2, gr * GH:(gr + 1) * GH, :], start=True, stop=True)
                    last.then_inc(kv_made.sem, 1)
                scan(1)
                if late is not None:
                    pe.wait_ge(kv_masked.sem, kv_masked.after(c, B))
                    pe.wait_ge(at_done.sem, at_done.after(c, TILES))
                    late_experts(4, 6, 1)
                tpose_set(c, T_WO, at_done)
                pe.wait_ge(tcopied[T_WO].sem, tcopied[T_WO].after(c, 1))
                if late is not None:
                    pe.wait_ge(acc_done[1].sem, acc_done[1].after(late, TILES * 5))
                for tile in range(TILES):
                    for k in range(KD):
                        last = pe.matmul(OB[1][:, tile * D:(tile + 1) * D], fT[:, k, tile * P:(tile + 1) * P],
                                         g["wo"][:, k, :], start=(k == 0), stop=(k == KD - 1))
                last.then_inc(wo_made.sem, 1)
                scan(1)
                if late is not None:
                    pe.wait_ge(xr_done.sem, xr_done.after(c, 1))
                    late_experts(6, 8, 1)
                scan(PAIRS - at_pair[0])
                mlp_input(c)
                if i is not None:
                    scan_output(i, PAIRS - 2)
                if late is None:
                    pe.wait_ge(kv_masked.sem, kv_masked.after(c, B))
                mlp_first(c, 0)
                if i is not None:
                    scan_output(i, PAIRS - 1)

            step(0, None, None)
            step(1, 0, None)
            with pe.Fori(2, CHUNKS) as i:
                step(i, i - 1, i - 2)
            step(None, CHUNKS - 1, CHUNKS - 2)
            step(None, None, CHUNKS - 1)

        @block.vector
        def _(dve):
            dve.wait_ge(g["back_in"], BACK_IN)
            dve.wait_ge(pool_set.sem, POOL_SETS)
            dve.wait_ge(c_in.sem, 16)
            dve.tensor_scalar(decay[:], g["a_log"][:], -5.0, 2.0, ALU.max, ALU.min).then_inc(set_up.sem, 1)
            dve.wait_ge(exp_done.sem, 1)
            dve.tensor_scalar(decay[:], decay[:], -1.0, None, ALU.mult).then_inc(set_up.sem, 1)
            dve.wait_ge(set_up.sem, 2)
            dve.memset(decayed_state[:, 0:HALF], 0.0).then_inc(stepped.sem, 1)
            dve.memset(decayed_state[:, HALF:D], 0.0).then_inc(stepped.sem, 1)

            def set_cblk(i, q):
                for j in range(QT // YSTEPS):
                    t0 = q * QT + j * YSTEPS
                    place = cblk[:, t0 * YROWS:t0 * YROWS + YSTEPS * (YROWS + B)].rearrange("p (t c) -> p t c", c=YROWS + B)
                    dve.tensor_tensor(place[:, :, 0:B],
                                      cT[:, bass.ds(i * CT + t0, YSTEPS)].unsqueeze(2).broadcast_to([P, YSTEPS, B]),
                                      g["own_batch"][:].unsqueeze(1).broadcast_to([P, YSTEPS, B]), ALU.mult).then_inc(cblk_set.sem, 1)

            def wait_apart(signal_, value):
                dve.wait_ge(signal_.sem, value)
                dve.nop(nofuse=True)

            def scan_pair(i, n):
                for s in (2 * n, 2 * n + 1):
                    for h in range(2):
                        part = slice(h * HALF, (h + 1) * HALF)
                        dve.wait_ge(stepped.sem, stepped.after(i, 2 * (s - 1) + h + 1))
                        dve.tensor_tensor(decayed_state[:, part], state[:, (s - 1) % RING, part], decay[:, part],
                                          ALU.mult).then_inc(decayed.sem, 1)
                    if s == 2 * n:
                        dve.wait_ge(u_made.sem, u_made.after(i, n + 1))
                        if not (isinstance(i, int) and i == 0 and n < 4):
                            dve.wait_ge(y_made.sem, y_made.after(i, n - 3))
                    for h in range(2):
                        part = slice(h * HALF, (h + 1) * HALF)
                        wait_apart(decayed, decayed.after(i, 2 * s + h + 1))
                        dve._custom_dve(add_sat, out=state[:, s % RING, part], in0=decayed_state[:, part],
                                        in1=U[n % 2][:, s % 2 * D + h * HALF:s % 2 * D + (h + 1) * HALF],
                                        s0=LIMIT, s1=-LIMIT).then_inc(stepped.sem, 1)
                q, at = divmod(n, PAIRS // QUARTERS)
                if at == 4:
                    if q == 0:
                        dve.wait_ge(y_made.sem, y_made.after(i, 0))
                        set_cblk(i, QUARTERS - 1)
                    else:
                        dve.wait_ge(y_made.sem, y_made.after(i, PAIRS // QUARTERS * q))
                        set_cblk(i + 1, q - 1)

            def step(i, c, late):
                at_pair = [0]

                def scan(pairs):
                    for _ in range(pairs if i is not None else 0):
                        scan_pair(i, at_pair[0])
                        at_pair[0] += 1

                def ln_stats(c, k, src, done, n_done):
                    for tile in range(TILES):
                        dve.wait_ge(done.sem, done.after(c, n_done[tile]))
                        dve.bn_stats(stats[:, tile], src[:, tile]).then_inc(bn_done[k].sem, 1)
                    for tile in range(TILES):
                        wait_apart(bn_done[k], bn_done[k].after(c, tile + 1))
                        dve.bn_aggr(mv[:, k, tile], stats[:, tile]).then_inc(aggr_done[k].sem, 1)

                def ln_apply(c, k, src, dst, done):
                    dve.wait_ge(rstd_done[k].sem, rstd_done[k].after(c, 1))
                    for tile in range(TILES):
                        dve.tensor_scalar(dst[:, tile], src[:, tile], mv[:, k, tile, 0:1], rstd[:, k, tile:tile + 1],
                                          ALU.subtract, ALU.mult).then_inc(done.sem, 1)

                def ln_affine(k, src, scale, bias, dst, done):
                    dve.wait_ge(aggr_done[k].sem, aggr_done[k].after(c, TILES))
                    for tile in range(TILES):
                        dve.scalar_tensor_tensor(out=dst[:, tile], in0=src[:, tile], scalar=mv[:, k, tile, 0:1],
                                                 in1=rows[scale][:], op0=ALU.subtract, op1=ALU.mult).then_inc(u_done[k].sem, 1)
                    dve.wait_ge(rstd_done[k].sem, rstd_done[k].after(c, 1))
                    for tile in range(TILES):
                        dve.wait_ge(u_done[k].sem, u_done[k].after(c, tile + 1))
                        dve.scalar_tensor_tensor(out=dst[:, tile], in0=dst[:, tile], scalar=rstd[:, k, tile:tile + 1],
                                                 in1=bias(tile), op0=ALU.mult, op1=ALU.add).then_inc(done.sem, 1)

                def routing(c, f):
                    dve.wait_ge(gated[f].sem, gated[f].after(c, 1))
                    dve.tensor_tensor(score[:], TB[:, 0:TILES * E].rearrange("p (i e) -> p i e", i=TILES),
                                      g["gate_b"][:].unsqueeze(1).broadcast_to([P, TILES, E]), ALU.add).then_inc(route[f].sem, 1)
                    dve.wait_ge(route[f].sem, route[f].after(c, 1))
                    grid = [P, E, E]
                    steps = (
                        lambda i_, e_, f_, gt, ge: dve.tensor_tensor(gt, f_, e_, ALU.is_gt),
                        lambda i_, e_, f_, gt, ge: dve.tensor_tensor(ge, f_, e_, ALU.is_equal),
                        lambda i_, e_, f_, gt, ge: dve.tensor_tensor(ge, ge, g["before"][:].rearrange("p (e f) -> p e f", e=E), ALU.mult),
                        lambda i_, e_, f_, gt, ge: dve.tensor_tensor(gt, gt, ge, ALU.add),
                        lambda i_, e_, f_, gt, ge: dve.tensor_reduce(rank[:, i_], gt, AX.X, ALU.add),
                        lambda i_, e_, f_, gt, ge: dve.tensor_scalar(rank[:, i_], rank[:, i_], 1.5, None, ALU.is_lt),
                        lambda i_, e_, f_, gt, ge: dve.tensor_tensor(comb[:, f, i_], rank[:, i_], score[:, i_], ALU.mult),
                    )
                    for n, step in enumerate(steps):
                        for tile in range(TILES):
                            e_ = score[:, tile].unsqueeze(2).broadcast_to(grid)
                            f_ = score[:, tile].unsqueeze(1).broadcast_to(grid)
                            gt = above[:, tile].rearrange("p (e f) -> p e f", e=E)
                            ge = level[:, tile].rearrange("p (e f) -> p e f", e=E)
                            if n >= 2:
                                dve.wait_ge(route[f].sem, route[f].after(c, 1 + TILES * (n - 1) + tile + 1))
                            step(tile, e_, f_, gt, ge).then_inc(comb_done[f].sem if n == 6 else route[f].sem, 1)

                def set_acc(c, f, dst, src):
                    dve.wait_ge(bias_made[f].sem, bias_made[f].after(c, 1))
                    dve.tensor_tensor(dst[:].rearrange("p i d -> p (i d)"), TB[:], src[:].rearrange("p i d -> p (i d)"),
                                      ALU.add).then_inc(acc_set[f].sem, 1)

                def add_expert(c, f, e, dst):
                    dve.wait_ge(expert_out[f].sem, expert_out[f].after(c, e + 1))
                    if e == 0:
                        dve.wait_ge(acc_set[f].sem, acc_set[f].after(c, 1))
                        dve.wait_ge(comb_done[f].sem, comb_done[f].after(c, TILES))
                    for tile in range(TILES):
                        if e:
                            dve.wait_ge(acc_done[f].sem, acc_done[f].after(c, TILES * (e - 1) + tile + 1))
                        dve.scalar_tensor_tensor(out=dst[:, tile], in0=OB[(e + 1) % 2][:, tile * D:(tile + 1) * D],
                                                 scalar=comb[:, f, tile, e:e + 1], in1=dst[:, tile],
                                                 op0=ALU.mult, op1=ALU.add).then_inc(acc_done[f].sem, 1)

                def late_experts(first, end, scans):
                    for e in range(first, end):
                        scan(scans)
                        add_expert(late, 1, e, x3)

                scan(2)
                if c is not None:
                    dve.wait_ge(y_tposed.sem, y_tposed.after(c, 1))
                    dve.wait_ge(tok_in.sem, tok_in.after(c, 16 * 3 * B))
                    dve.tensor_tensor(gT[:].rearrange("p k b t -> p k t b"), TB[:].rearrange("p (k t b) -> p k t b", k=KD, b=B),
                                      z_t[:].rearrange("p k b t -> p k t b"), ALU.mult).then_inc(y_gated.sem, 1)
                scan(1)
                if c is not None:
                    dve.wait_ge(mamba_out.sem, mamba_out.after(c, 1))
                    dve.wait_ge(xnb_done.sem, xnb_done.after(c, 1))
                    dve.tensor_tensor(h_t[:].rearrange("p i d -> p (i d)"), OB[0][:], xnb[:].rearrange("p i d -> p (i d)"),
                                      ALU.add).then_inc(h_done.sem, 1)
                    ln_stats(c, MAMBA, h_t, h_done, (1, 1))
                    dve.wait_ge(xb_done.sem, xb_done.after(c, 1))
                    ln_affine(MAMBA, h_t, "ln_w", lambda tile: xb[:, tile], x1, x1_done)
                    ln_stats(c, FFN1, x1, x1_done, (1, 2))
                scan(1)
                if c is not None:
                    ln_apply(c, FFN1, x1, turn, xf_done[0])
                scan(2)
                if late is not None:
                    dve.wait_ge(mlp_made.sem, mlp_made.after(late, 1))
                    dve.wait_ge(mb_done.sem, mb_done.after(late, 2))
                    dve.wait_ge(stored.sem, stored.after(late, 0))
                    dve.tensor_tensor(x3[:].rearrange("p i d -> p (i d)"), OB[1][:], mb[:].rearrange("p i d -> p (i d)"),
                                      ALU.add).then_inc(x3_done.sem, 1)
                    ln_stats(late, FFN2, x3, x3_done, (1, 1))
                if c is not None:
                    routing(c, 0)
                if late is not None:
                    ln_apply(late, FFN2, x3, late_turn, xf_done[1])
                scan(1)
                if c is not None:
                    set_acc(c, 0, acc, x1)
                for e in range(E):
                    scan(1)
                    if c is not None:
                        add_expert(c, 0, e, acc)
                    if late is not None:
                        if e == 0:
                            routing(late, 1)
                        if e == COMB_AFTER + 1:
                            set_acc(late, 1, x3, x3)
                if c is not None:
                    ln_stats(c, OUTER, acc, acc_done[0], (TILES * (E - 1) + 1, TILES * E))
                    ln_apply(c, OUTER, acc, a_t, a_done)
                    ln_stats(c, LN1, a_t, a_done, (1, 2))
                    ln_affine(LN1, a_t, "ln1_s", lambda tile: rows["ln1_b"][:], turn, xl_done)
                if late is not None:
                    late_experts(0, 4, 1)
                if c is None:
                    if late is not None:
                        late_experts(4, 8, 1)
                    else:
                        scan(PAIRS - at_pair[0])
                    return
                scan(1)
                for bs, made, dst, done in ((HB, k_made, kT, kT_done), (OB, q_made, qT, qT_done)):
                    for j in range(2):
                        dve.wait_ge(made.sem, made.after(c, j + 1))
                        dve.tensor_scalar(dst[:, 2 * j:2 * j + 2].rearrange("p k q -> p (k q)"), bs[j][:], 0.0,
                                          g["feature_eps"][:, 0:1], ALU.max, ALU.add).then_inc(done.sem, 1)
                    if done is kT_done:
                        scan(1)
                for tile in range(TILES):
                    SB = (HB[0], HB[1], TB, OB[1])
                    if tile:
                        dve.wait_ge(num_made.sem, num_made.after(c, tile))
                    for hh in range(GH):
                        dve.wait_ge(scored.sem, scored.after(c, GH * tile + hh + 1))
                        dve.tensor_tensor(ss[:, hh], SB[hh][:].rearrange("p (g q) -> p g q", g=GROUPS),
                                          g["causal"][:].unsqueeze(1).broadcast_to([P, GROUPS, P]), ALU.mult).then_inc(masked.sem, 1)
                    scan(2)
                    dve.wait_ge(num_made.sem, num_made.after(c, tile + 1))
                    num = OB[0][:, 0:H * HV].rearrange("p (h v) -> p h v", h=H)
                    dve.reciprocal(rec[:, tile], num[:, :, DH]).then_inc(rec_done.sem, 1)
                    dve.wait_ge(rec_done.sem, rec_done.after(c, tile + 1))
                    dve.tensor_tensor(turn[:, tile].rearrange("p (h m) -> p h m", h=H), num[:, :, 0:DH],
                                      rec[:, tile].unsqueeze(2).broadcast_to([P, H, DH]), ALU.mult).then_inc(at_done.sem, 1)
                for b in range(B):
                    dve.wait_ge(kv_made.sem, kv_made.after(c, b + 1))
                    if b == 0:
                        dve.wait_ge(kv_added.sem, kv_added.after(c, 0))
                    dve.tensor_tensor(kvm[:, b], HB[b % 2][:, 0:H * HV], g["own_head"][:], ALU.mult).then_inc(kv_masked.sem, 1)
                scan(1)
                if late is not None:
                    late_experts(4, 6, 1)
                scan(1)
                dve.wait_ge(wo_made.sem, wo_made.after(c, 1))
                dve.tensor_tensor(xr[:].rearrange("p i d -> p (i d)"), OB[1][:], a_t[:].rearrange("p i d -> p (i d)"),
                                  ALU.add).then_inc(xr_done.sem, 1)
                ln_stats(c, LN2, xr, xr_done, (1, 1))
                ln_affine(LN2, xr, "ln2_s", lambda tile: rows["ln2_b"][:], late_turn, yl_done)
                if late is not None:
                    late_experts(6, 8, 1)
                if i is not None:
                    scan(PAIRS - at_pair[0])

            for q in range(QUARTERS - 1):
                set_cblk(0, q)
            step(0, None, None)
            step(1, 0, None)
            with dve.Fori(2, CHUNKS) as i:
                step(i, i - 1, i - 2)
            step(None, CHUNKS - 1, CHUNKS - 2)
            step(None, None, CHUNKS - 1)


def lay_out(x):
    def per_partition(v):
        return np.ascontiguousarray(np.asarray(v).reshape(-1, P).T)

    def blocks(w):
        w = np.asarray(w)
        return np.ascontiguousarray(w.reshape(-1, P, w.shape[1]).transpose(1, 0, 2))

    def row(v):
        return np.ascontiguousarray(np.broadcast_to(np.asarray(v).reshape(1, -1), (P, np.asarray(v).size)))

    def padded(w):
        w = np.asarray(w)
        full = np.zeros((D, H, PADH), w.dtype)
        full[:, :, :DH] = w
        return blocks(full.reshape(D, H * PADH))

    a = {k[len("L0_"):]: np.asarray(v) for k, v in x.items()}
    conv = a["attn_a_conv_w"][:, 0, :].reshape(KD, P, TAPS).transpose(1, 0, 2)
    a_log = np.tile(a["attn_a_A_log"].T, (B, 1))
    return {
        "x": a["attn_a_x"],
        "in_w": blocks(a["attn_a_in_w"].T), "in_b": per_partition(a["attn_a_in_b"]),
        "conv_w": np.ascontiguousarray(conv), "conv_b": per_partition(a["attn_a_conv_b"]),
        "b_w": blocks(a["attn_a_B_w"].T), "b_b": row(a["attn_a_B_b"]),
        "c_w": blocks(a["attn_a_C_w"].T), "c_b": a["attn_a_C_b"].reshape(-1, 1),
        "a_log": np.ascontiguousarray(a_log),
        "out_w": blocks(a["attn_a_out_w"].T), "out_b": row(a["attn_a_out_b"]),
        "ln_w": row(a["attn_a_ln_w"]), "ln_b": row(a["attn_a_ln_b"]),
        "ln1_s": row(a["attn_b_ln1_scale"]), "ln1_b": row(a["attn_b_ln1_bias"]),
        "ln2_s": row(a["attn_b_ln2_scale"]), "ln2_b": row(a["attn_b_ln2_bias"]),
        "mlp_b2": row(a["attn_b_b2"]),
        "wq": padded(a["attn_b_wq"]), "wk": padded(a["attn_b_wk"]),
        "wv": blocks(a["attn_b_wv"].reshape(D, D)), "wo": blocks(a["attn_b_wo"].reshape(D, D)),
        "m_w1": blocks(a["attn_b_w1"]), "m_b1": per_partition(a["attn_b_b1"]), "m_w2": blocks(a["attn_b_w2"]),
        "gate_w": blocks(a["ffn_gate_w"]), "gate_b": row(a["ffn_gate_b"]),
        "f_w1": np.ascontiguousarray(a["ffn_w1"].reshape(E, KD, P, F).transpose(2, 0, 1, 3)),
        "f_b1": np.ascontiguousarray(a["ffn_b1"].reshape(E, F // P, P).transpose(2, 0, 1)),
        "f_w2": np.ascontiguousarray(a["ffn_w2"].reshape(E, F // P, P, D).transpose(2, 0, 1, 3)),
        "f_b2": a["ffn_b2"],
        **constants(),
    }


def kernel(**inputs):
    import concourse.bacc as bacc
    from concourse.bass_utils import run_bass_kernel_spmd

    arrays = lay_out(inputs)
    nc = bacc.Bacc("TRN2", target_bir_lowering=False, num_devices=1)
    names = {n: nc.dram_tensor(f"in_{n}", a.shape, mybir.dt.from_np(a.dtype), kind="ExternalInput").ap()
             for n, a in arrays.items()}
    out = nc.dram_tensor("out_0", (B, L, D), mybir.dt.float32, kind="ExternalOutput").ap()
    build(nc, names, out)
    r = run_bass_kernel_spmd(nc, [{f"in_{n}": a for n, a in arrays.items()}], core_ids=[0])
    return r.results[0]["out_0"]
```

```python
import numpy as np
import concourse.bass as bass
from concourse import mybir
from contextlib import ExitStack

B, L, D = 4, 1024, 256
N_STATE = 32
TAPS = 4
H, DH = 16, 16
MLP = 1024
E, F = 8, 256
P = 128
KD = D // P
CT = 64
CHUNKS = L // CT
TILES = B * CT // P
TOK = B * CT
UNITS = 8
PARTS = 4
QT = CT // UNITS
UPAIRS = QT // 2
PAIRS = CT // 2
YSTEPS = QT
YROWS = YSTEPS * B
RING = 8
SPLITS = 4
ROWS = SPLITS * B
PADH = 32
GROUPS = H * PADH // P
GH = H // GROUPS
HV = DH + 1
LIMIT = 10.0
KERNEL_EPS = 0.001
HALF = D // 2


def constants():
    p = np.arange(P)
    ident = np.eye(P, dtype=np.float32)
    same = (p[:, None] // CT) == (p[None, :] // CT)
    causal = (same & (p[:, None] <= p[None, :])).astype(np.float32)
    own_head = np.zeros((P, GROUPS, GH, HV), np.float32)
    for hh in range(GH):
        own_head[PADH * hh:PADH * hh + DH, :, hh, :] = 1.0
    feature_eps = np.where(p % PADH < DH, KERNEL_EPS, 0.0).astype(np.float32)[:, None]
    own_batch = (p[:, None] // N_STATE == np.arange(B)[None, :]).astype(np.float32)
    before = np.tile((np.arange(E)[None, :] < np.arange(E)[:, None]).astype(np.float32)[None], (P, 1, 1))
    return {
        "ident": ident, "causal": causal, "own_head": own_head.reshape(P, -1),
        "feature_eps": feature_eps, "own_batch": own_batch, "before": before.reshape(P, -1),
    }


def build(nc, t, out):
    f32, f32r = mybir.dt.float32, mybir.dt.float32r
    ALU = mybir.AluOpType
    ACT = mybir.ActivationFunctionType
    AX = mybir.AxisListType
    add_sat = bass.dve_ops.TENSOR_ADD_SAT

    ctx = ExitStack()
    with ctx:
        def sb(name, shape, dt=f32, where=ctx):
            return where.enter_context(nc.sbuf_tensor(name, shape, dt))

        def sem(name, where=ctx):
            return where.enter_context(nc.semaphore(name))

        def scratch(name, shape, dt=f32):
            return nc.dram_tensor(name, shape, dt, kind="Internal").ap()

        xn_dram = scratch("xn_dram", (B, L, D))
        z_dram = scratch("z_dram", (B, P, KD, L))
        xs_dram = scratch("xs_dram", (2, B, L, D))
        bs_dram = scratch("bs_dram", (SPLITS, B, L, N_STATE))
        c_dram = scratch("c_dram", (B, N_STATE, L))

        def weight(name, shape):
            return sb(name + "_sb", shape)

        lows = {}

        def split_weight(name, shape):
            with ExitStack() as shared:
                whole = sb(name + "_sb", shape, where=shared)
            lows[name] = sb(name + "_lo", shape, f32r)
            return whole

        ident = weight("ident", [P, P])
        a_log = weight("a_log", [P, D])
        own_batch = weight("own_batch", [P, B])
        out_w = weight("out_w", [P, KD, D])
        rows = {n: weight(n, [P, D]) for n in
                ("out_b", "ln_w", "ln_b", "ln1_s", "ln1_b", "ln2_s", "ln2_b", "mlp_b2")}
        gate_w = weight("gate_w", [P, KD, E])
        gate_b = weight("gate_b", [P, E])
        before = weight("before", [P, E * E])
        f_w1 = split_weight("f_w1", [P, E, KD, F])
        f_b1 = weight("f_b1", [P, E, F // P])
        f_w2 = split_weight("f_w2", [P, E, F // P, D])
        f_b2 = weight("f_b2", [E, D])
        wq = weight("wq", [P, KD, GROUPS * P])
        wk = weight("wk", [P, KD, GROUPS * P])
        wv = weight("wv", [P, KD, D])
        wo = weight("wo", [P, KD, D])
        m_w1 = split_weight("m_w1", [P, KD, MLP])
        m_b1 = weight("m_b1", [P, MLP // P])
        m_w2 = split_weight("m_w2", [P, MLP // P, D])
        causal = weight("causal", [P, P])
        own_head = weight("own_head", [P, GROUPS * GH * HV])
        feature_eps = weight("feature_eps", [P, 1])
        back = [("a_log", a_log), ("own_batch", own_batch), ("out_w", out_w), *rows.items(),
                ("gate_w", gate_w), ("gate_b", gate_b), ("before", before), ("f_w1", f_w1), ("f_b1", f_b1),
                ("f_w2", f_w2), ("f_b2", f_b2), ("wq", wq), ("wk", wk), ("wv", wv), ("wo", wo),
                ("m_w1", m_w1), ("m_b1", m_b1), ("m_w2", m_w2), ("causal", causal), ("own_head", own_head),
                ("feature_eps", feature_eps)]

        bank = [ctx.enter_context(nc.psum_tensor(f"bank{i}", [P, 512], f32)) for i in range(8)]

        front_in = sem("front_in")
        back_in = sem("back_in")
        BACK_IN = 16 * len(back)

        front_part(nc, t, locals())
        main_part(nc, t, out, locals())


def front_part(nc, t, g):
    f32, f32r = mybir.dt.float32, mybir.dt.float32r
    ALU = mybir.AluOpType
    ACT = mybir.ActivationFunctionType
    bank, ident = g["bank"], g["ident"]
    front_in = g["front_in"]
    NT = L // P
    LH = L // 2
    GR = NT // 2

    with ExitStack() as own:
        def sb(name, shape, dt=f32):
            return own.enter_context(nc.sbuf_tensor(name, shape, dt))

        def sem(name):
            return own.enter_context(nc.semaphore(name))

        in_w = sb("in_w_sb", [P, KD, 2 * D])
        in_b = sb("in_b_sb", [P, 2 * KD])
        conv_w = sb("conv_w_sb", [P, KD, TAPS])
        conv_b = sb("conv_b_sb", [P, KD])
        b_w = sb("b_w_sb", [P, KD, N_STATE])
        c_w = sb("c_w_sb", [P, KD, N_STATE])
        c_b = sb("c_b_sb", [N_STATE, 1])
        b_b = sb("b_b_sb", [P, N_STATE])
        front = [("ident", ident), ("in_w", in_w), ("in_b", in_b), ("conv_w", conv_w), ("conv_b", conv_b),
                 ("b_w", b_w), ("c_w", c_w), ("c_b", c_b), ("b_b", b_b)]
        FRONT_IN = 16 * len(front)
        xt = sb("xt", [P, NT, D])
        xn = sb("xn", [P, NT, D])
        stats = sb("stats", [P, NT, 6])
        mv = sb("mv", [P, NT, 2])
        ve = sb("ve", [P, NT])
        rstd = sb("rstd", [P, NT])
        eps = sb("eps", [P, NT])
        mhalf = sb("mhalf", [P, NT])
        xnT = sb("xnT", [P, KD, L])
        xaT = sb("xaT", [P, KD, L + 3])
        zT = sb("zT", [P, KD, L])
        cv = sb("cv", [P, KD, L])
        xcT = sb("xcT", [P, KD, L])
        xhi = sb("xhi", [P, NT, D], f32r)
        xlo = sb("xlo", [P, NT, D], f32r)
        bt = sb("bt", [P, NT, N_STATE])
        bhi = sb("bhi", [P, NT, N_STATE], f32r)
        blo = sb("blo", [P, NT, N_STATE], f32r)
        cT = sb("cT", [N_STATE, L])

        x_in = sem("x_in")
        pads_set = sem("pads_set")
        stat_done = sem("stat_done")
        aggr_done = sem("aggr_done")
        ve_done = sem("ve_done")
        rstd_done = sem("rstd_done")
        ln_done = sem("ln_done")
        xn_out = sem("xn_out")
        tp_done = sem("tp_done")
        tp_copied = sem("tp_copied")
        proj_done = sem("proj_done")
        z_read = sem("z_read")
        xa_read = sem("xa_read")
        z_out = sem("z_out")
        conv_step = sem("conv_step")
        conv_done = sem("conv_done")
        silu_done = sem("silu_done")
        back_done = sem("back_done")
        hi_done = sem("hi_done")
        lo_done = sem("lo_done")
        xs_out = sem("xs_out")
        bmm_done = sem("bmm_done")
        bt_done = sem("bt_done")
        bhi_done = sem("bhi_done")
        blo_done = sem("blo_done")
        bs_out = sem("bs_out")
        cmm_done = sem("cmm_done")
        cT_done = sem("cT_done")
        c_out = sem("c_out")
        NPROJ = 2 * 2 * KD
        PRIMED = 1
        primed = (xn_out, tp_done, silu_done, xs_out, bs_out, conv_done, z_out, back_done, cmm_done, c_out, lo_done, cT_done, bt_done)

        BACK = (bank[0], bank[1], bank[7])

        block = own.enter_context(nc.Block())

        @block.sync
        def _(sp):
            def wait_apart(sem_, value):
                sp.wait_ge(sem_, value)
                sp.nop(nofuse=True)

            def load_x(b):
                if not (isinstance(b, int) and b == 0):
                    wait_apart(ln_done, NT * b)
                sp.dma_start(xt[:], t["x"][bass.ds(b, 1)].rearrange("b (i p) d -> p (b i) d", p=P)).then_inc(x_in, 16)

            def store_xn(b):
                wait_apart(ln_done, NT * (b + 1))
                sp.dma_start(g["xn_dram"][bass.ds(b, 1)].rearrange("b (i p) d -> p (b i) d", p=P), xn[:]).then_inc(xn_out, 16)

            def store_z(b):
                wait_apart(z_read, NPROJ // 2 * (b + 1))
                sp.dma_start(g["z_dram"][bass.ds(b, 1)].rearrange("b p k t -> p (b k) t"), zT[:]).then_inc(z_out, 16)

            def store_scan_operands(b):
                wait_apart(lo_done, PRIMED + NT * (b + 1))
                wait_apart(hi_done, NT * (b + 1))
                for s, tile in enumerate((xhi, xlo)):
                    sp.dma_start(g["xs_dram"][s, bass.ds(b, 1)].rearrange("b (i p) d -> p (b i) d", p=P), tile[:].bitcast(f32)).then_inc(xs_out, 16)
                wait_apart(blo_done, b + 1)
                wait_apart(bhi_done, b + 1)
                for s, tile in enumerate((bhi, bhi, blo, blo)):
                    sp.dma_start(g["bs_dram"][s, bass.ds(b, 1)].rearrange("b (i p) n -> p (b i) n", p=P), tile[:].bitcast(f32)).then_inc(bs_out, 16)
                wait_apart(cT_done, PRIMED + 2 * (b + 1))
                sp.dma_start(g["c_dram"][bass.ds(b, 1)].rearrange("b n t -> (b n) t"), cT[:]).then_inc(c_out, 16)

            load_x(0)
            for n, tile in front:
                sp.dma_start(tile[:], t[n]).then_inc(front_in, 16)
            store_xn(0)
            load_x(1)
            store_z(0)
            for n, tile in g["back"]:
                sp.dma_start(tile[:], t[n]).then_inc(g["back_in"], 16)
            with sp.Fori(0, B - 2) as b:
                store_xn(b + 1)
                load_x(b + 2)
                store_z(b + 1)
                store_scan_operands(b)
            store_xn(B - 1)
            store_z(B - 1)
            store_scan_operands(B - 2)
            store_scan_operands(B - 1)
            sp.wait_ge(xn_out, PRIMED + 16 * B)
            sp.wait_ge(z_out, PRIMED + 16 * B)
            sp.wait_ge(xs_out, PRIMED + 32 * B)
            sp.wait_ge(bs_out, PRIMED + 64 * B)
            sp.wait_ge(c_out, PRIMED + 16 * B)

        @block.vector
        def _(dve):
            dve.memset(xaT[:, :, 0:2], 0.0).then_inc(pads_set, 1)
            dve.memset(xaT[:, :, L + 2:L + 3], 0.0).then_inc(pads_set, 1)

            def norm(b):
                dve.wait_ge(x_in, 16 * (b + 1))
                for i in range(NT):
                    dve.bn_stats(stats[:, i, :], xt[:, i, :]).then_inc(stat_done, 1)
                dve.wait_ge(stat_done, NT * (b + 1))
                dve.nop(nofuse=True)
                for i in range(NT):
                    dve.bn_aggr(mv[:, i, :], stats[:, i, :]).then_inc(aggr_done, 1)
                dve.wait_ge(rstd_done, b + 1)
                dve.wait_ge(xn_out, PRIMED + 16 * b)
                dve.wait_ge(tp_done, PRIMED + NT // 2 * b)
                for i in range(NT):
                    dve.tensor_scalar(xn[:, i, :], xt[:, i, :], mv[:, i, 0:1], rstd[:, i:i + 1],
                                      ALU.subtract, ALU.mult).then_inc(ln_done, 1)

            def conv(b):
                dve.wait_ge(front_in, FRONT_IN)
                dve.wait_ge(xa_read, NPROJ // 2 * (b + 1))
                dve.wait_ge(silu_done, PRIMED + KD * b)
                for k in range(KD):
                    dve.tensor_scalar(cv[:, k, :], xaT[:, k, 0:L], conv_w[:, k, 0:1], conv_b[:, k:k + 1],
                                      ALU.mult, ALU.add).then_inc(conv_step, 1)
                for j in range(1, TAPS):
                    for k in range(KD):
                        dve.wait_ge(conv_step, (TAPS - 1) * KD * b + KD * (j - 1) + k + 1)
                        step = dve.scalar_tensor_tensor(out=cv[:, k, :], in0=xaT[:, k, j:j + L], scalar=conv_w[:, k, j:j + 1],
                                                        in1=cv[:, k, :], op0=ALU.mult, op1=ALU.add)
                        step.then_inc(conv_step if j < TAPS - 1 else conv_done, 1)
                for i in range(NT):
                    if i == 0:
                        dve.wait_ge(xs_out, PRIMED + 32 * b)
                    dve.wait_ge(hi_done, NT * b + i + 1)
                    dve.tensor_tensor(xlo[:, i, :], BACK[i % 3][:, 0:D], xhi[:, i, :].bitcast(f32), ALU.subtract).then_inc(lo_done, 1)
                dve.wait_ge(bmm_done, b + 1)
                dve.tensor_tensor(bt[:], bank[6][:, 0:NT * N_STATE].rearrange("p (i n) -> p i n", i=NT),
                                  b_b[:].unsqueeze(1).broadcast_to([P, NT, N_STATE]), ALU.add).then_inc(bt_done, 1)
                dve.wait_ge(bhi_done, b + 1)
                dve.wait_ge(bs_out, PRIMED + 64 * b)
                dve.tensor_tensor(blo[:], bt[:], bhi[:].bitcast(f32), ALU.subtract).then_inc(blo_done, 1)

            dve.wait_ge(pads_set, 4)
            norm(0)
            with dve.Fori(0, B - 1) as b:
                norm(b + 1)
                conv(b)
            conv(B - 1)

        @block.gpsimd
        def _(pool):
            for s in primed:
                pool.sem_inc(s, PRIMED)
            pool.memset(eps[:], 1e-5).then_inc(pads_set, 1)
            pool.memset(mhalf[:], -0.5).then_inc(pads_set, 1)
            pool.wait_ge(pads_set, 4)
            with pool.Fori(0, B) as b:
                pool.wait_ge(aggr_done, NT * (b + 1))
                pool.tensor_tensor(ve[:], mv[:, :, 1], eps[:], ALU.add).then_inc(ve_done, 1)
                pool.wait_ge(ve_done, b + 1)
                pool.tensor_tensor(rstd[:], ve[:], mhalf[:], ALU.pow).then_inc(rstd_done, 1)

        @block.scalar
        def _(act):
            act.wait_ge(front_in, FRONT_IN)

            def project_z(b):
                for i in range(NT // 2):
                    act.wait_ge(tp_done, PRIMED + NT // 2 * b + i + 1)
                    act.activation(xnT[:, :, 2 * P * i:2 * P * (i + 1)].rearrange("p k (i q) -> p k i q", i=2),
                                   bank[i % 2][:].rearrange("p (i k q) -> p k i q", i=2, k=KD), ACT.Copy).then_inc(tp_copied, 1)
                act.wait_ge(z_out, PRIMED + 16 * b)
                for h in range(2):
                    for k in range(KD):
                        act.wait_ge(proj_done, NPROJ * b + KD * h + k + 1)
                        act.activation(zT[:, k, LH * h:LH * (h + 1)], bank[2 + KD * h + k][:], ACT.Silu,
                                       bias=in_b[:, KD + k:KD + k + 1]).then_inc(z_read, 1)

            def project_x(b):
                for h in range(2):
                    for k in range(KD):
                        act.wait_ge(proj_done, NPROJ * b + NPROJ // 2 + KD * h + k + 1)
                        act.activation(xaT[:, k, 2 + LH * h:2 + LH * (h + 1)], bank[2 + KD * h + k][:], ACT.Identity,
                                       bias=in_b[:, k:k + 1]).then_inc(xa_read, 1)

            def silu(b):
                act.wait_ge(back_done, PRIMED + NT * b)
                act.wait_ge(cmm_done, PRIMED + 2 * b)
                for k in range(KD):
                    act.wait_ge(conv_done, PRIMED + KD * b + k + 1)
                    act.activation(xcT[:, k, :], cv[:, k, :], ACT.Silu).then_inc(silu_done, 1)

            def parts(b):
                act.wait_ge(xs_out, PRIMED + 32 * b)
                for i in range(NT):
                    act.wait_ge(back_done, PRIMED + NT * b + i + 1)
                    act.activation(xhi[:, i, :], BACK[i % 3][:, 0:D], ACT.Copy).then_inc(hi_done, 1)
                act.wait_ge(bs_out, PRIMED + 64 * b)
                act.wait_ge(bt_done, PRIMED + b + 1)
                act.activation(bhi[:], bt[:], ACT.Copy).then_inc(bhi_done, 1)
                act.wait_ge(c_out, PRIMED + 16 * b)
                for h in range(2):
                    act.wait_ge(cmm_done, PRIMED + 2 * b + h + 1)
                    act.activation(cT[:, LH * h:LH * (h + 1)], bank[4 + h][0:N_STATE, :], ACT.Identity,
                                   bias=c_b[:, 0:1]).then_inc(cT_done, 1)

            project_z(0)
            project_x(0)
            with act.Fori(0, B - 1) as b:
                project_z(b + 1)
                silu(b)
                project_x(b + 1)
                parts(b)
            silu(B - 1)
            parts(B - 1)

        @block.tensor
        def _(pe):
            pe.wait_ge(front_in, FRONT_IN)

            def project(b):
                first = isinstance(b, int)
                if not first:
                    pe.wait_ge(lo_done, PRIMED + NT * (b - 1))
                for i in range(NT // 2):
                    for j in range(2):
                        pe.wait_ge(ln_done, NT * b + 2 * i + j + 1)
                        if i >= 2:
                            pe.wait_ge(tp_copied, NT // 2 * b + i - 1)
                        for k in range(KD):
                            last = pe.transpose(bank[i % 2][:, (KD * j + k) * P:(KD * j + k + 1) * P],
                                                xn[:, 2 * i + j, k * P:(k + 1) * P], ident[:])
                    last.then_inc(tp_done, 1)
                for part in range(2):
                    for h in range(2):
                        if part == 0:
                            pe.wait_ge(tp_copied, NT // 2 * b + NT // 4 * (h + 1))
                        for m in range(KD):
                            n = KD * h + m
                            if part == 0 and n == 0 and not first:
                                pe.wait_ge(cT_done, PRIMED + 2 * (b - 1))
                            if part:
                                pe.wait_ge(z_read, NPROJ // 2 * b + n + 1)
                            elif not first:
                                pe.wait_ge(xa_read, NPROJ // 2 * b)
                            row = (KD if part == 0 else 0) + m
                            for k in range(KD):
                                last = pe.matmul(bank[2 + n][:], in_w[:, k, row * P:(row + 1) * P],
                                                 xnT[:, k, LH * h:LH * (h + 1)], start=(k == 0), stop=(k == KD - 1))
                            last.then_inc(proj_done, 1)

            def scan_operands(b):
                pe.wait_ge(silu_done, PRIMED + KD * (b + 1))
                for i in range(NT):
                    if i >= 3:
                        pe.wait_ge(lo_done, PRIMED + NT * b + i - 2)
                    for k in range(KD):
                        last = pe.transpose(BACK[i % 3][:, k * P:(k + 1) * P], xcT[:, k, i * P:(i + 1) * P], ident[:])
                    last.then_inc(back_done, 1)
                pe.wait_ge(bt_done, PRIMED + b)
                for i in range(NT):
                    for k in range(KD):
                        last = pe.matmul(bank[6][:, i * N_STATE:(i + 1) * N_STATE], xcT[:, k, i * P:(i + 1) * P],
                                         b_w[:, k, :], start=(k == 0), stop=(k == KD - 1))
                last.then_inc(bmm_done, 1)
                if not isinstance(b, int):
                    pe.wait_ge(xa_read, NPROJ // 2 * (b + 2))
                for h in range(2):
                    for k in range(KD):
                        last = pe.matmul(bank[4 + h][0:N_STATE, :], c_w[:, k, :], xcT[:, k, LH * h:LH * (h + 1)],
                                         start=(k == 0), stop=(k == KD - 1))
                    last.then_inc(cmm_done, 1)

            project(0)
            with pe.Fori(0, B - 1) as b:
                project(b + 1)
                scan_operands(b)
            scan_operands(B - 1)


class Signal:

    def __init__(self, sem, per_chunk, before=0):
        self.sem, self.per_chunk, self.before = sem, per_chunk, before

    def after(self, chunk, n):
        return chunk * self.per_chunk + (n + self.before)


def main_part(nc, t, out, g):
    f32, f32r = mybir.dt.float32, mybir.dt.float32r
    ALU = mybir.AluOpType
    ACT = mybir.ActivationFunctionType
    AX = mybir.AxisListType
    add_sat = g["add_sat"]
    bank, ident, rows = g["bank"], g["ident"], g["rows"]
    BACK_IN = g["BACK_IN"]
    LNS = 6
    MAMBA, FFN1, OUTER, LN1, LN2, FFN2 = range(LNS)
    LN_EPS = {MAMBA: 1e-5, FFN1: 1e-5, OUTER: 1e-5, LN1: 1e-6, LN2: 1e-6, FFN2: 1e-5}
    TPOSES = 5
    T_FFN1, T_ATT, T_WO, T_MLP, T_FFN2 = range(TPOSES)
    PARTED = (T_FFN1, T_MLP, T_FFN2)

    HI, LO = range(2)
    SPLIT = ("f_w1", "f_w2", "m_w1", "m_w2")

    with ExitStack() as own:
        def sb(name, shape, dt=f32):
            return own.enter_context(nc.sbuf_tensor(name, shape, dt))

        def signal(name, per_chunk, before=0):
            return Signal(own.enter_context(nc.semaphore(name)), per_chunk, before)

        def signals(name, count, per_chunk, before=0):
            return [signal(f"{name}{k}", per_chunk, before) for k in range(count)]

        decay = sb("decay", [P, D])
        xrows = sb("xrows", [P, QT, D], f32r)
        brows = sb("brows", [P, QT, B, N_STATE], f32r)
        cT = sb("cT_all", [P, L + CT])
        cblk = sb("cblk", [P, PARTS * QT * YROWS + YROWS])
        decayed_state = sb("decayed_state", [P, D])
        state = sb("state", [P, RING, D])
        x_t = sb("x_t", [P, TILES, D])
        xn_t = sb("xn_t", [P, TILES, D])
        z_t = sb("z_t", [P, KD, B, CT])
        turn = sb("turn", [P, TILES, D])
        late_turn = sb("late_turn", [P, TILES, D])
        res = sb("res", [P, TILES, D])
        a_t = sb("a_t", [P, TILES, D])
        mb = sb("mb", [P, TILES, D])
        x3 = sb("x3", [P, TILES, D])
        stats = sb("m_stats", [P, TILES, 6])
        mv = sb("m_mv", [P, LNS, TILES, 2])
        ve = sb("m_ve", [P, LNS, TILES])
        rstd = sb("m_rstd", [P, LNS, TILES])
        eps = sb("m_eps", [P, LNS, TILES])
        mhalf = sb("m_mhalf", [P, TILES])
        fT = turn[:].rearrange("p i (j q) -> p (i j) q", j=1)
        late_fT = late_turn[:].rearrange("p i (j q) -> p (i j) q", j=1)
        with ExitStack() as shared:
            kT = shared.enter_context(nc.sbuf_tensor("kT", [P, GROUPS, TOK], f32))
        fT_parts = sb("fT_parts", [P, 2, KD, TOK], f32r)
        late_fT_parts = sb("late_fT_parts", [P, 2, KD, TOK], f32r)
        score = sb("score", [P, TILES, E])
        above = sb("above", [P, TILES, E * E])
        level = sb("level", [P, TILES, E * E])
        rank = sb("rank", [P, TILES, E])
        comb = sb("comb", [P, 2, TILES, E])
        combT = sb("combT", [E, TOK])
        with ExitStack() as shared:
            ss = shared.enter_context(nc.sbuf_tensor("ss", [P, GH, GROUPS, P], f32))
        hs_parts = sb("hs_parts", [P, 2, 2, F // P, TOK], f32r)
        hs_whole = sb("hs_whole", [P, 2, F // P, TOK])
        qT = sb("qT", [P, GROUPS, TOK])
        ktok = hs_whole[:].rearrange("p s m q -> p s (m q)")
        vv = sb("vv", [P, TILES, H, HV])
        kv = sb("kv", [P, B, GROUPS * GH * HV])
        kvm = sb("kvm", [P, 2, GROUPS * GH * HV])
        rec = sb("rec", [P, TILES, H])
        whi = {n: sb(n + "_hi", [P, g[n].shape[1] * g[n].shape[2] * (g[n].shape[3] if len(g[n].shape) > 3 else 1)], f32r)
               for n in SPLIT}

        def flat(name, where=g):
            return where[name][:].rearrange("p e k f -> p (e k f)" if len(g[name].shape) > 3 else "p k f -> p (k f)")

        def weights(name):
            lo = g["lows"][name][:]
            if len(g[name].shape) > 3:
                hi = whi[name][:].rearrange("p (e k f) -> p e k f", e=g[name].shape[1], k=g[name].shape[2])
            else:
                hi = whi[name][:].rearrange("p (k f) -> p k f", k=g[name].shape[1])
            return hi, lo

        f_w1, f_w2, m_w1, m_w2 = (weights(n) for n in SPLIT)
        PRODUCTS = ((HI, HI), (HI, LO), (LO, HI))
        U, Y, HB, OB, TB = [bank[0], bank[1]], bank[2], [bank[3], bank[4]], [bank[5], bank[6]], bank[7]

        ROW_DMAS = 2 + B
        rows_in = [signal(f"rows_in{q}", 2 * 16 * ROW_DMAS) for q in range(PARTS)]
        c_in = signal("c_in", 0)
        tok_in = signal("tok_in", 16 * 3 * B)
        stored = signal("stored", 16 * B, before=1)
        set_up = signal("set_up", 0)
        decayed = signal("decayed", 2 * CT)
        stepped = signal("stepped", 2 * CT, before=2)
        cblk_set = signal("cblk_set", UNITS)
        y_gated = signal("y_gated", 1)
        h_done = signal("h_done", 1)
        bn_done = signals("bn_done", LNS, TILES)
        aggr_done = signals("aggr_done", LNS, TILES)
        u_done = {k: signal(f"u_done{k}", TILES) for k in (MAMBA, LN1, LN2)}
        x1_done = signal("x1_done", TILES)
        xf_done = signals("xf_done", 2, TILES)
        route = signals("route", 2, 1 + TILES * 6)
        comb_done = signals("comb_done", 2, TILES)
        acc_set = signals("acc_set", 2, 1)
        acc_done = signals("acc_done", 2, E * TILES, before=1)
        a_done = signal("a_done", TILES)
        xl_done = signal("xl_done", TILES)
        kT_done = signal("kT_done", 2)
        qT_done = signal("qT_done", 2)
        masked = signal("masked", TILES * GH)
        kv_masked = signal("kv_masked", B)
        rec_done = signal("rec_done", TILES)
        at_done = signal("at_done", TILES)
        xr_done = signal("xr_done", 1)
        yl_done = signal("yl_done", TILES)
        x3_done = signal("x3_done", 1)
        u_made = signal("u_made", PAIRS)
        y_made = signal("y_made", PAIRS)
        y_tposed = signal("y_tposed", 1)
        mamba_out = signal("mamba_out", 1)
        tposed = signals("tposed", TPOSES, 1)
        gated = signals("gated", 2, 1)
        comb_tposed = signals("comb_tposed", 2, 1)
        bias_made = signals("bias_made", 2, 1)
        hidden = signals("hidden", 2, E)
        expert_out = signals("expert_out", 2, E)
        k_made = signal("k_made", 2)
        q_made = signal("q_made", 2)
        v_made = signal("v_made", 1)
        k_tposed = signal("k_tposed", TILES)
        scored = signal("scored", TILES * GH)
        num_made = signal("num_made", TILES)
        kv_made = signal("kv_made", B)
        wo_made = signal("wo_made", 1)
        mlp_hidden = signal("mlp_hidden", 4)
        mlp_made = signal("mlp_made", 1)
        exp_done = signal("exp_done", 0)
        y_copied = signal("y_copied", 1, before=1)
        tcopied = signals("tcopied", TPOSES, 1)
        comb_copied = signals("comb_copied", 2, 1)
        tcopied_hi = {k: signal(f"tcopied_hi{k}", 1) for k in PARTED}
        relued = signals("relued", 2, E * (F // P))
        relued_hi = signals("relued_hi", 2, E * (F // P))
        gelued_hi = signal("gelued_hi", MLP // P)
        weights_hi = signal("weights_hi", 0)
        v_copied = signal("v_copied", TILES)
        k_copied = signal("k_copied", TILES)
        gelued = signal("gelued", MLP // P)
        pool_set = signal("pool_set", 0)
        xn_biased = signal("xn_biased", 1)
        x_biased = signal("x_biased", 1)
        ve_done = signals("ve_done", LNS, 1)
        rstd_done = signals("rstd_done", LNS, 1)
        kv_added = signal("kv_added", B, before=1)
        mb_done = signal("mb_done", 2)
        weights_lo = signal("weights_lo", 0)
        t_lo = {k: signal(f"t_lo{k}", 1) for k in PARTED}
        relu_lo = signals("relu_lo", 2, E * (F // P))
        gelu_lo = signal("gelu_lo", MLP // P)
        primed = (*acc_done, y_copied, kv_added, stored)
        POOL_SETS = 9 + LNS
        TURN_AFTER, GATE_AFTER, COMB_AFTER, BIAS_AFTER = 1, 2, 4, 5

        block = own.enter_context(nc.Block())

        def load_rows(sp, chunk, u):
            t0 = chunk * CT + u * QT
            q = u % PARTS
            for j in range(2):
                sp.dma_start(xrows[32 * q + 2 * B * j:32 * q + 2 * B * (j + 1)].bitcast(f32),
                             g["xs_dram"][:, :, bass.ds(t0, QT), :].rearrange("s b t d -> (s b) t d")).then_inc(rows_in[q].sem, 16)
            for b in range(B):
                sp.dma_start(brows[32 * q + b:32 * q + ROWS:B, :, b, :].bitcast(f32),
                             g["bs_dram"][:, b, bass.ds(t0, QT), :]).then_inc(rows_in[q].sem, 16)

        def load_tokens(sp, chunk):
            for b in range(B):
                p0 = (b % 2) * CT
                rows_of = (slice(p0, p0 + CT), b // 2)
                sp.dma_start(x_t[rows_of], t["x"][b, bass.ds(chunk * CT, CT), :]).then_inc(tok_in.sem, 16)
                sp.dma_start(xn_t[rows_of], g["xn_dram"][b, bass.ds(chunk * CT, CT), :]).then_inc(tok_in.sem, 16)
                sp.dma_start(z_t[:, :, b, :], g["z_dram"][b, :, :, bass.ds(chunk * CT, CT)]).then_inc(tok_in.sem, 16)

        @block.sync
        def _(sp):
            sp.dma_start(cT[:, 0:L], g["c_dram"].rearrange("b n t -> (b n) t")).then_inc(c_in.sem, 16)
            sp.wait_ge(pool_set.sem, POOL_SETS)
            for u in range(PARTS):
                load_rows(sp, 0, u)
            sp.wait_ge(g["back_in"], BACK_IN)

            def wait_apart(signal_, value):
                sp.wait_ge(signal_.sem, value)
                sp.nop(nofuse=True)

            def chunk_loads(i, more):
                load_tokens(sp, i)
                for u in range(UNITS if more else UNITS - PARTS):
                    wait_apart(u_made, u_made.after(i, UPAIRS * (u + 1)))
                    load_rows(sp, i + (u + PARTS) // UNITS, (u + PARTS) % UNITS)

            def store(c):
                for b in range(B):
                    p0 = (b % 2) * CT
                    sp.dma_start(out[b, bass.ds(c * CT, CT), :], x3[p0:p0 + CT, b // 2]).then_inc(stored.sem, 16)

            def tokens_free(c):
                wait_apart(mamba_out, mamba_out.after(c, 1))
                wait_apart(h_done, h_done.after(c, 1))
                wait_apart(x1_done, x1_done.after(c, TILES))

            def finish(c):
                wait_apart(acc_done[1], acc_done[1].after(c, E * TILES))
                store(c)

            chunk_loads(0, True)
            tokens_free(0)
            chunk_loads(1, True)
            with sp.Fori(2, CHUNKS - 1) as i:
                tokens_free(i - 1)
                chunk_loads(i, True)
                finish(i - 2)
            tokens_free(CHUNKS - 2)
            chunk_loads(CHUNKS - 1, False)
            for c in range(CHUNKS - 3, CHUNKS):
                finish(c)
            sp.wait_ge(stored.sem, stored.after(CHUNKS - 1, 16 * B))

        @block.gpsimd
        def _(pool):
            for s in primed:
                pool.sem_inc(s.sem, 1)
            pool.memset(brows[:].bitcast(f32), 0.0).then_inc(pool_set.sem, 1)
            pool.memset(cblk[:], 0.0).then_inc(pool_set.sem, 1)
            pool.memset(cT[:, L:L + CT], 0.0).then_inc(pool_set.sem, 1)
            pool.memset(mhalf[:], -0.5).then_inc(pool_set.sem, 1)
            for k, value in LN_EPS.items():
                pool.memset(eps[:, k], value).then_inc(pool_set.sem, 1)
            pool.memset(kv[:], 0.0).then_inc(pool_set.sem, 1)
            pool.memset(vv[:], 1.0).then_inc(pool_set.sem, 1)
            pool.memset(state[:, RING - 1], 0.0).then_inc(pool_set.sem, 1)
            pool.memset(ve[:], 0.0).then_inc(pool_set.sem, 1)
            pool.memset(rstd[:], 0.0).then_inc(pool_set.sem, 1)
            pool.wait_ge(pool_set.sem, POOL_SETS)
            pool.wait_ge(g["back_in"], BACK_IN)

            def rstd_of(c, k):
                pool.wait_ge(aggr_done[k].sem, aggr_done[k].after(c, TILES))
                pool.tensor_tensor(ve[:, k], mv[:, k, :, 1], eps[:, k], ALU.add).then_inc(ve_done[k].sem, 1)
                pool.wait_ge(ve_done[k].sem, ve_done[k].after(c, 1))
                pool.tensor_tensor(rstd[:, k], ve[:, k], mhalf[:], ALU.pow).then_inc(rstd_done[k].sem, 1)

            def both(row):
                return rows[row][:].unsqueeze(1).broadcast_to([P, TILES, D])

            def low(lo, whole, hi):
                return pool.tensor_tensor(lo, whole, hi.bitcast(f32), ALU.subtract)

            def low_set(c, k):
                whole, parts = (late_turn, late_fT_parts) if k in (T_MLP, T_FFN2) else (turn, fT_parts)
                pool.wait_ge(tcopied[k].sem, tcopied[k].after(c, 1))
                pool.wait_ge(tcopied_hi[k].sem, tcopied_hi[k].after(c, 1))
                low(parts[:, LO], whole[:], parts[:, HI]).then_inc(t_lo[k].sem, 1)

            def low_relu(c, f, e):
                for m in range(F // P):
                    n = F // P * e + m + 1
                    pool.wait_ge(relued_hi[f].sem, relued_hi[f].after(c, n))
                    pool.wait_ge(relued[f].sem, relued[f].after(c, n))
                    low(hs_parts[:, LO, e % 2, m], hs_whole[:, e % 2, m], hs_parts[:, HI, e % 2, m]).then_inc(relu_lo[f].sem, 1)

            def low_gelu(c, j):
                for m in range(2):
                    pool.wait_ge(gelued_hi.sem, gelued_hi.after(c, 2 * j + m + 1))
                    pool.wait_ge(gelued.sem, gelued.after(c, 2 * j + m + 1))
                    low(hs_parts[:, LO, j % 2, m], hs_whole[:, j % 2, m], hs_parts[:, HI, j % 2, m]).then_inc(gelu_lo.sem, 1)

            def add_kv(c, tile):
                for b in (2 * tile, 2 * tile + 1):
                    pool.wait_ge(kv_masked.sem, kv_masked.after(c, b + 1))
                    pool.tensor_tensor(kv[:, b], kv[:, b], kvm[:, b % 2], ALU.add).then_inc(kv_added.sem, 1)

            def step(c, late):
                if late is not None:
                    low_set(late, T_MLP)
                if c is not None:
                    pool.wait_ge(tok_in.sem, tok_in.after(c, 16 * 3 * B))
                    pool.tensor_tensor(xn_t[:], xn_t[:], both("out_b"), ALU.add).then_inc(xn_biased.sem, 1)
                    pool.tensor_tensor(x_t[:], x_t[:], both("ln_b"), ALU.add).then_inc(x_biased.sem, 1)
                if late is not None:
                    low_gelu(late, 0)
                    low_gelu(late, 1)
                if c is not None:
                    rstd_of(c, MAMBA)
                if late is not None:
                    low_gelu(late, 2)
                if c is not None:
                    rstd_of(c, FFN1)
                if late is not None:
                    low_gelu(late, 3)
                if c is not None:
                    low_set(c, T_FFN1)
                    low_relu(c, 0, 0)
                    low_relu(c, 0, 1)
                if late is not None:
                    rstd_of(late, FFN2)
                if c is not None:
                    low_relu(c, 0, 2)
                if late is not None:
                    low_set(late, T_FFN2)
                if c is not None:
                    for e in range(3, E):
                        low_relu(c, 0, e)
                if late is not None:
                    low_relu(late, 1, 0)
                if c is not None:
                    rstd_of(c, OUTER)
                if late is not None:
                    low_relu(late, 1, 1)
                if c is not None:
                    rstd_of(c, LN1)
                if late is not None:
                    for e in range(2, 4):
                        low_relu(late, 1, e)
                if c is not None:
                    if late is not None:
                        pool.wait_ge(x3_done.sem, x3_done.after(late, 1))
                    pool.wait_ge(acc_done[0].sem, acc_done[0].after(c, TILES * E))
                    pool.tensor_tensor(mb[:], res[:], both("mlp_b2"), ALU.add).then_inc(mb_done.sem, 1)
                    add_kv(c, 0)
                if late is not None:
                    low_relu(late, 1, 4)
                    low_relu(late, 1, 5)
                if c is not None:
                    add_kv(c, 1)
                    rstd_of(c, LN2)
                if late is not None:
                    low_relu(late, 1, 6)
                    low_relu(late, 1, 7)
                if c is not None:
                    pool.wait_ge(xr_done.sem, xr_done.after(c, 1))
                    pool.wait_ge(mb_done.sem, mb_done.after(c, 1))
                    pool.tensor_tensor(mb[:], mb[:], a_t[:], ALU.add).then_inc(mb_done.sem, 1)

            for k, name in enumerate(SPLIT):
                pool.wait_ge(weights_hi.sem, k + 1)
                low(flat(name, g["lows"]), flat(name), whi[name][:]).then_inc(weights_lo.sem, 1)
            step(0, None)
            with pool.Fori(2, CHUNKS) as i:
                step(i - 1, i - 2)
            step(CHUNKS - 1, CHUNKS - 2)
            step(None, CHUNKS - 1)

        @block.scalar
        def _(act):
            act.wait_ge(set_up.sem, 1)
            act.activation(decay[:], decay[:], ACT.Exp).then_inc(exp_done.sem, 1)
            act.wait_ge(g["back_in"], BACK_IN)
            act.wait_ge(pool_set.sem, POOL_SETS)

            for name in SPLIT:
                act.activation(whi[name][:], flat(name), ACT.Copy).then_inc(weights_hi.sem, 1)

            def copy_set(c, k):
                act.wait_ge(tposed[k].sem, tposed[k].after(c, 1))
                whole, parts = (late_turn, late_fT_parts) if k in (T_MLP, T_FFN2) else (turn, fT_parts)
                act.activation(whole[:].rearrange("p k q -> p (k q)"), TB[:], ACT.Copy).then_inc(tcopied[k].sem, 1)
                if k in PARTED:
                    act.activation(parts[:, HI].rearrange("p k q -> p (k q)"), TB[:],
                                   ACT.Copy).then_inc(tcopied_hi[k].sem, 1)

            def relu(c, f, e):
                act.wait_ge(hidden[f].sem, hidden[f].after(c, e + 1))
                for m in range(F // P):
                    for slot, done in ((hs_parts[:, HI, e % 2], relued_hi[f]), (hs_whole[:, e % 2], relued[f])):
                        act.activation(slot[:, m], HB[e % 2][:, m * TOK:(m + 1) * TOK],
                                       ACT.Relu, bias=g["f_b1"][:, e, m:m + 1]).then_inc(done.sem, 1)

            def copy_comb(c, f):
                act.wait_ge(comb_tposed[f].sem, comb_tposed[f].after(c, 1))
                act.activation(combT[:], TB[0:E, 0:TOK], ACT.Copy).then_inc(comb_copied[f].sem, 1)

            def copy_k(c, tile):
                act.wait_ge(k_tposed.sem, k_tposed.after(c, tile + 1))
                act.activation(ktok[:, tile], OB[tile][:], ACT.Copy).then_inc(k_copied.sem, 1)

            def gelu(late, j):
                if late is None:
                    return
                act.wait_ge(mlp_hidden.sem, mlp_hidden.after(late, j + 1))
                for m in range(2):
                    for slot, done in ((hs_parts[:, HI, j % 2], gelued_hi), (hs_whole[:, j % 2], gelued)):
                        act.activation(slot[:, m], HB[j % 2][:, m * TOK:(m + 1) * TOK],
                                       ACT.Gelu_apprx_tanh, bias=g["m_b1"][:, 2 * j + m:2 * j + m + 1]).then_inc(done.sem, 1)

            def step(c, late):
                if late is not None:
                    copy_set(late, T_MLP)
                gelu(late, 0)
                if c is not None:
                    act.wait_ge(y_made.sem, y_made.after(c, PAIRS))
                    act.activation(turn[:].rearrange("p i d -> p (i d)"), Y[:], ACT.Copy).then_inc(y_copied.sem, 1)
                for j in range(1, 4):
                    gelu(late, j)
                if c is not None:
                    copy_set(c, T_FFN1)
                    relu(c, 0, 0)
                    relu(c, 0, 1)
                    copy_comb(c, 0)
                    relu(c, 0, 2)
                if late is not None:
                    copy_set(late, T_FFN2)
                if c is not None:
                    for e in range(3, E):
                        relu(c, 0, e)
                        if e == COMB_AFTER + 1 and late is not None:
                            copy_comb(late, 1)
                if late is not None:
                    if c is None:
                        copy_comb(late, 1)
                    for e in range(4):
                        relu(late, 1, e)
                if c is not None:
                    copy_set(c, T_ATT)
                    act.wait_ge(v_made.sem, v_made.after(c, 1))
                    for n in range(TILES):
                        act.activation(vv[:, n, :, 0:DH], TB[:, n * D:(n + 1) * D].rearrange("p (h m) -> p h m", h=H),
                                       ACT.Copy).then_inc(v_copied.sem, 1)
                    copy_k(c, 0)
                if late is not None:
                    relu(late, 1, 4)
                    relu(late, 1, 5)
                if c is not None:
                    copy_k(c, 1)
                    copy_set(c, T_WO)
                if late is not None:
                    relu(late, 1, 6)
                    relu(late, 1, 7)

            step(0, None)
            with act.Fori(2, CHUNKS) as i:
                step(i - 1, i - 2)
            step(CHUNKS - 1, CHUNKS - 2)
            step(None, CHUNKS - 1)

        @block.tensor
        def _(pe):
            pe.wait_ge(g["back_in"], BACK_IN)
            pe.wait_ge(pool_set.sem, POOL_SETS)
            pe.wait_ge(exp_done.sem, 1)

            def scan_inputs(i, n):
                u, first = divmod(n, UPAIRS)
                q = u % PARTS
                if first == 0:
                    pe.wait_ge(rows_in[q].sem, rows_in[q].after(i, 16 * ROW_DMAS * (u // PARTS + 1)))
                if not (isinstance(i, int) and i == 0 and n < 2):
                    pe.wait_ge(stepped.sem, stepped.after(i, 4 * (n - 1)))
                for j in range(2):
                    tq = (2 * n + j) % QT
                    last = pe.matmul(U[n % 2][:, j * D:(j + 1) * D], brows[32 * q:32 * q + ROWS, tq].rearrange("r b n -> r (b n)"),
                                     xrows[32 * q:32 * q + ROWS, tq, :], start=True, stop=True)
                last.then_inc(u_made.sem, 1)

            def scan_output(i, n):
                if n == 0:
                    pe.wait_ge(y_copied.sem, y_copied.after(i, 0))
                if n % UPAIRS == 0:
                    pe.wait_ge(cblk_set.sem, cblk_set.after(i, n // UPAIRS + 1))
                pe.wait_ge(stepped.sem, stepped.after(i, 4 * (n + 1)))
                for s in (2 * n, 2 * n + 1):
                    tile, row = divmod(s // YSTEPS * YROWS, P)
                    slot = s % (PARTS * QT)
                    last = pe.matmul(Y[row:row + YROWS, tile * D:(tile + 1) * D], cblk[:, slot * YROWS:(slot + 1) * YROWS],
                                     state[:, s % RING, :], start=(s % YSTEPS == 0), stop=(s % YSTEPS == YSTEPS - 1),
                                     tile_position=(0, row))
                last.then_inc(y_made.sem, 1)

            def step(i, c, late):
                at_pair = [0]

                def scan(pairs):
                    for _ in range(pairs if i is not None else 0):
                        n = at_pair[0]
                        if n + 1 < PAIRS:
                            scan_inputs(i, n + 1)
                        if n >= 2:
                            scan_output(i, n - 2)
                        at_pair[0] += 1

                def transposes(src):
                    for tile in range(TILES):
                        for kk in range(KD):
                            last = pe.transpose(TB[:, kk * TOK + tile * P:kk * TOK + (tile + 1) * P],
                                                src[:, tile, kk * P:(kk + 1) * P], ident[:])
                    return last

                def tpose_set(c, k, done):
                    pe.wait_ge(done.sem, done.after(c, TILES))
                    transposes(late_turn if k in (T_MLP, T_FFN2) else turn).then_inc(tposed[k].sem, 1)

                def gate(c, f):
                    k_set, src = ((T_FFN1, fT), (T_FFN2, late_fT))[f]
                    pe.wait_ge(tcopied[k_set].sem, tcopied[k_set].after(c, 1))
                    pe.wait_ge(tcopied_hi[k_set].sem, tcopied_hi[k_set].after(c, 1))
                    for tile in range(TILES):
                        for k in range(KD):
                            last = pe.matmul(TB[:, tile * E:(tile + 1) * E], src[:, k, tile * P:(tile + 1) * P],
                                             g["gate_w"][:, k, :], start=(k == 0), stop=(k == KD - 1))
                    last.then_inc(gated[f].sem, 1)

                def turn_comb(c, f):
                    pe.wait_ge(comb_done[f].sem, comb_done[f].after(c, TILES))
                    for tile in range(TILES):
                        last = pe.transpose(TB[0:E, tile * P:(tile + 1) * P], comb[:, f, tile, :], ident[:])
                    last.then_inc(comb_tposed[f].sem, 1)

                def bias(c, f):
                    pe.wait_ge(comb_copied[f].sem, comb_copied[f].after(c, 1))
                    for tile in range(TILES):
                        last = pe.matmul(TB[:, tile * D:(tile + 1) * D], combT[:, tile * P:(tile + 1) * P],
                                         g["f_b2"][:], start=True, stop=True)
                    last.then_inc(bias_made[f].sem, 1)

                def split_product(hi_done, lo_done, dst, data, w, tiles, ks, stationary):
                    for n, (dp, wp) in enumerate(PRODUCTS):
                        if n == 0:
                            pe.wait_ge(*hi_done)
                        elif dp == LO:
                            pe.wait_ge(*lo_done)
                        for tile in range(tiles):
                            for k in range(ks):
                                d_, w_ = data(dp, k, tile), w(wp, k, tile)
                                first = n == 0 and k == 0 and tile == 0
                                last = pe.matmul(dst(tile), *((w_, d_) if stationary == "w" else (d_, w_)),
                                                 start=first and stationary != "more",
                                                 stop=(n == len(PRODUCTS) - 1 and k == ks - 1), skip_group_check=True)
                    return last

                def first_products(c, k_set, bank_, w, parts):
                    return split_product(
                        (tcopied_hi[k_set].sem, tcopied_hi[k_set].after(c, 1)), (t_lo[k_set].sem, t_lo[k_set].after(c, 1)),
                        lambda m: bank_[:, m * TOK:(m + 1) * TOK], lambda p, k, m: parts[:, p, k, :], w, 2, KD, "w")

                def second_products(hi_done, lo_done, bank_, slot, w, more=False):
                    return split_product(
                        hi_done, lo_done, lambda tile: bank_[:, tile * D:(tile + 1) * D],
                        lambda p, m, tile: hs_parts[:, p, slot, m, tile * P:(tile + 1) * P], w, TILES, F // P,
                        "more" if more else "data")

                def first_layer(c, f, e):
                    if e >= 2:
                        pe.wait_ge(relued[f].sem, relued[f].after(c, F // P * (e - 1)))
                    first_products(c, (T_FFN1, T_FFN2)[f], HB[e % 2],
                                   lambda p, k, m: f_w1[p][:, e, k, m * P:(m + 1) * P],
                                   (fT_parts, late_fT_parts)[f]).then_inc(hidden[f].sem, 1)

                def second_layer(c, f, e):
                    if e >= 2:
                        pe.wait_ge(acc_done[f].sem, acc_done[f].after(c, TILES * (e - 1)))
                    second_products((relued_hi[f].sem, relued_hi[f].after(c, F // P * (e + 1))),
                                    (relu_lo[f].sem, relu_lo[f].after(c, F // P * (e + 1))), OB[(e + 1) % 2], e % 2,
                                    lambda p, m, tile: f_w2[p][:, e, m, :]).then_inc(expert_out[f].sem, 1)

                def mlp_input(c):
                    tpose_set(c, T_MLP, yl_done)

                def mlp_first(c, j):
                    if c is None:
                        return
                    if j >= 2:
                        pe.wait_ge(gelued.sem, gelued.after(c, 2 * (j - 1)))
                    first_products(c, T_MLP, HB[j % 2], lambda p, k, m: m_w1[p][:, k, (2 * j + m) * P:(2 * j + m + 1) * P],
                                   late_fT_parts).then_inc(mlp_hidden.sem, 1)

                def mlp_second(j):
                    if late is None:
                        return
                    last = second_products((gelued_hi.sem, gelued_hi.after(late, 2 * (j + 1))),
                                           (gelu_lo.sem, gelu_lo.after(late, 2 * (j + 1))), OB[1], j % 2,
                                           lambda p, m, tile: m_w2[p][:, 2 * j + m, :], more=j > 0)
                    if j == 3:
                        last.then_inc(mlp_made.sem, 1)

                def late_experts(first, end, made=0):
                    for e in range(first + made, first + 2):
                        first_layer(late, 1, e)
                    for e in range(first, end):
                        if first < e < end - 1:
                            first_layer(late, 1, e + 1)
                        if e not in (2, 3):
                            scan(1)
                        if c is not None and e == 0:
                            pe.wait_ge(acc_done[0].sem, acc_done[0].after(c, TILES * (E - 1)))
                        elif c is not None and e == 1:
                            pe.wait_ge(acc_done[0].sem, acc_done[0].after(c, TILES * E))
                        elif c is not None and e == 6:
                            pe.wait_ge(xr_done.sem, xr_done.after(c, 1))
                        if c is not None and e == E - 1:
                            mlp_input(c)
                        second_layer(late, 1, e)

                if i is not None:
                    scan_inputs(i, 0)
                scan(1)
                mlp_first(late, 1)
                if late is not None:
                    pe.wait_ge(acc_done[1].sem, acc_done[1].after(late, 0))
                if c is not None:
                    pe.wait_ge(y_copied.sem, y_copied.after(c, 1))
                    transposes(turn).then_inc(y_tposed.sem, 1)
                scan(1)
                mlp_second(0)
                if c is not None:
                    pe.wait_ge(y_gated.sem, y_gated.after(c, 1))
                    for tile in range(TILES):
                        for k in range(KD):
                            last = pe.matmul(OB[0][:, tile * D:(tile + 1) * D],
                                             z_t[:, k, 2 * tile:2 * tile + 2, :], g["out_w"][:, k, :],
                                             start=(k == 0), stop=(k == KD - 1))
                    last.then_inc(mamba_out.sem, 1)
                mlp_first(late, 2)
                mlp_second(1)
                scan(1)
                mlp_first(late, 3)
                mlp_second(2)
                if c is not None:
                    tpose_set(c, T_FFN1, xf_done[0])
                scan(1)
                mlp_second(3)
                scan(1)
                if c is not None:
                    if late is None:
                        pe.wait_ge(weights_lo.sem, len(SPLIT))
                    gate(c, 0)
                    first_layer(c, 0, 0)
                    first_layer(c, 0, 1)
                scan(2)
                if c is not None:
                    turn_comb(c, 0)
                for e in range(E):
                    if c is not None:
                        if 1 <= e < E - 1:
                            first_layer(c, 0, e + 1)
                        if e:
                            scan(1)
                        if e == E - 1 and late is not None:
                            pe.wait_ge(relued[0].sem, relued[0].after(c, F // P * (E - 1)))
                            first_layer(late, 1, 0)
                        second_layer(c, 0, e)
                        if e == 0:
                            bias(c, 0)
                            scan(1)
                        if e == TURN_AFTER:
                            pe.wait_ge(acc_set[0].sem, acc_set[0].after(c, 1))
                    else:
                        scan(1)
                    if late is not None:
                        if e == TURN_AFTER:
                            tpose_set(late, T_FFN2, xf_done[1])
                        if e == GATE_AFTER:
                            gate(late, 1)
                        if e == COMB_AFTER:
                            turn_comb(late, 1)
                        if e == BIAS_AFTER:
                            bias(late, 1)
                if late is not None:
                    late_experts(0, 4, 0 if c is None else 1)
                    pe.wait_ge(acc_set[1].sem, acc_set[1].after(late, 1))
                if c is None:
                    if late is not None:
                        late_experts(4, 6)
                        late_experts(6, 8)
                        return
                    scan(PAIRS - at_pair[0])
                    scan_output(i, PAIRS - 2)
                    scan_output(i, PAIRS - 1)
                    return
                if late is None:
                    scan(2)
                tpose_set(c, T_ATT, xl_done)
                scan(1)
                pe.wait_ge(tcopied[T_ATT].sem, tcopied[T_ATT].after(c, 1))
                for w, bs, made in ((g["wk"], HB, k_made), (g["wq"], OB, q_made)):
                    if made is q_made and late is not None:
                        pe.wait_ge(acc_done[1].sem, acc_done[1].after(late, TILES * 4))
                    for gr in range(GROUPS):
                        for k in range(KD):
                            last = pe.matmul(bs[gr // 2][:, gr % 2 * TOK:(gr % 2 + 1) * TOK], w[:, k, gr * P:(gr + 1) * P],
                                             fT[:, k, :], start=(k == 0), stop=(k == KD - 1))
                        if gr % 2:
                            last.then_inc(made.sem, 1)
                    if made is k_made:
                        scan(1)
                for tile in range(TILES):
                    for k in range(KD):
                        last = pe.matmul(TB[:, tile * D:(tile + 1) * D], fT[:, k, tile * P:(tile + 1) * P],
                                         g["wv"][:, k, :], start=(k == 0), stop=(k == KD - 1))
                last.then_inc(v_made.sem, 1)
                scan(1)
                pe.wait_ge(kT_done.sem, kT_done.after(c, 2))
                pe.wait_ge(qT_done.sem, qT_done.after(c, 2))
                for tile in range(TILES):
                    SB = (HB[0], HB[1], TB, OB[1])
                    tok = slice(tile * P, (tile + 1) * P)
                    if tile and late is not None:
                        pe.wait_ge(acc_done[1].sem, acc_done[1].after(late, TILES * 5))
                    for gr in range(GROUPS):
                        last = pe.transpose(OB[tile][:, gr * P:(gr + 1) * P], kT[:, gr, tok], ident[:])
                    last.then_inc(k_tposed.sem, 1)
                    for hh in range(GH):
                        if hh == 3:
                            pe.wait_ge(k_copied.sem, k_copied.after(c, tile + 1))
                        elif tile and hh < 2:
                            pe.wait_ge(kv_masked.sem, kv_masked.after(c, hh + 1))
                        elif not tile and hh == 2:
                            pe.wait_ge(v_copied.sem, v_copied.after(c, TILES))
                        for gr in range(GROUPS):
                            last = pe.matmul(SB[hh][:, gr * P:(gr + 1) * P], kT[PADH * hh:PADH * (hh + 1), gr, tok],
                                             qT[PADH * hh:PADH * (hh + 1), gr, tok], start=True, stop=True)
                        last.then_inc(scored.sem, 1)
                        if hh == 1:
                            scan(1)
                    if tile:
                        pe.wait_ge(at_done.sem, at_done.after(c, tile))
                        if late is not None:
                            pe.wait_ge(acc_done[1].sem, acc_done[1].after(late, TILES * 6))
                    else:
                        pe.wait_ge(kv_added.sem, kv_added.after(c, 0))
                    W = GH * HV
                    for bb in range(2):
                        b = 2 * tile + bb
                        for gr in range(GROUPS):
                            pe.matmul(OB[0][CT * bb:CT * (bb + 1), gr * W:(gr + 1) * W],
                                      qT[:, gr, tile * P + CT * bb:tile * P + CT * (bb + 1)],
                                      kv[:, b, gr * W:(gr + 1) * W], start=(gr == 0), stop=False, skip_group_check=True)
                    scan(1)
                    for hh in range(GH):
                        pe.wait_ge(masked.sem, masked.after(c, GH * tile + hh + 1))
                        for gr in range(GROUPS):
                            hd = gr * GH + hh
                            last = pe.matmul(OB[0][:, hd * HV:(hd + 1) * HV], ss[:, hh, gr, :], vv[:, tile, hd, :],
                                             start=False, stop=(hh == GH - 1), skip_group_check=True)
                        if hh == 1:
                            scan(1)
                    last.then_inc(num_made.sem, 1)
                    for b in (2 * tile, 2 * tile + 1):
                        part = slice(CT * (b % 2), CT * (b % 2 + 1))
                        for gr in range(GROUPS):
                            last = pe.matmul(HB[b % 2][:, gr * W:(gr + 1) * W], ktok[part, tile, gr * P:(gr + 1) * P],
                                             vv[part, tile, gr * GH:(gr + 1) * GH, :], start=True, stop=True)
                        last.then_inc(kv_made.sem, 1)
                    if not tile:
                        scan(1)
                        if late is not None:
                            pe.wait_ge(kv_masked.sem, kv_masked.after(c, 2))
                            pe.wait_ge(at_done.sem, at_done.after(c, 1))
                            late_experts(4, 6)
                tpose_set(c, T_WO, at_done)
                scan(1)
                pe.wait_ge(tcopied[T_WO].sem, tcopied[T_WO].after(c, 1))
                for tile in range(TILES):
                    for k in range(KD):
                        last = pe.matmul(OB[1][:, tile * D:(tile + 1) * D], fT[:, k, tile * P:(tile + 1) * P],
                                         g["wo"][:, k, :], start=(k == 0), stop=(k == KD - 1))
                last.then_inc(wo_made.sem, 1)
                if late is not None:
                    pe.wait_ge(kv_masked.sem, kv_masked.after(c, B))
                    late_experts(6, 8)
                scan(PAIRS - at_pair[0])
                if late is None:
                    mlp_input(c)
                if i is not None:
                    scan_output(i, PAIRS - 2)
                if late is None:
                    pe.wait_ge(kv_masked.sem, kv_masked.after(c, B))
                mlp_first(c, 0)
                if i is not None:
                    scan_output(i, PAIRS - 1)

            step(0, None, None)
            step(1, 0, None)
            with pe.Fori(2, CHUNKS) as i:
                step(i, i - 1, i - 2)
            step(None, CHUNKS - 1, CHUNKS - 2)
            step(None, None, CHUNKS - 1)

        @block.vector
        def _(dve):
            dve.wait_ge(g["back_in"], BACK_IN)
            dve.wait_ge(pool_set.sem, POOL_SETS)
            dve.wait_ge(c_in.sem, 16)
            dve.tensor_scalar(decay[:], g["a_log"][:], -5.0, 2.0, ALU.max, ALU.min).then_inc(set_up.sem, 1)
            dve.wait_ge(exp_done.sem, 1)
            dve.tensor_scalar(decay[:], decay[:], -1.0, None, ALU.mult).then_inc(set_up.sem, 1)
            dve.wait_ge(set_up.sem, 2)
            dve.memset(decayed_state[:, 0:HALF], 0.0).then_inc(stepped.sem, 1)
            dve.memset(decayed_state[:, HALF:D], 0.0).then_inc(stepped.sem, 1)

            def set_cblk(i, u):
                slot = u % PARTS * QT
                place = cblk[:, slot * YROWS:slot * YROWS + YSTEPS * (YROWS + B)].rearrange("p (t c) -> p t c", c=YROWS + B)
                dve.tensor_tensor(place[:, :, 0:B],
                                  cT[:, bass.ds(i * CT + u * QT, YSTEPS)].unsqueeze(2).broadcast_to([P, YSTEPS, B]),
                                  g["own_batch"][:].unsqueeze(1).broadcast_to([P, YSTEPS, B]), ALU.mult).then_inc(cblk_set.sem, 1)

            def wait_apart(signal_, value):
                dve.wait_ge(signal_.sem, value)
                dve.nop(nofuse=True)

            def scan_pair(i, n):
                for s in (2 * n, 2 * n + 1):
                    for h in range(2):
                        part = slice(h * HALF, (h + 1) * HALF)
                        dve.wait_ge(stepped.sem, stepped.after(i, 2 * (s - 1) + h + 1))
                        dve.tensor_tensor(decayed_state[:, part], state[:, (s - 1) % RING, part], decay[:, part],
                                          ALU.mult).then_inc(decayed.sem, 1)
                    if s == 2 * n:
                        dve.wait_ge(u_made.sem, u_made.after(i, n + 1))
                        if not (isinstance(i, int) and i == 0 and n < 4):
                            dve.wait_ge(y_made.sem, y_made.after(i, n - 3))
                    for h in range(2):
                        part = slice(h * HALF, (h + 1) * HALF)
                        wait_apart(decayed, decayed.after(i, 2 * s + h + 1))
                        dve._custom_dve(add_sat, out=state[:, s % RING, part], in0=decayed_state[:, part],
                                        in1=U[n % 2][:, s % 2 * D + h * HALF:s % 2 * D + (h + 1) * HALF],
                                        s0=LIMIT, s1=-LIMIT).then_inc(stepped.sem, 1)
                u, at = divmod(n, UPAIRS)
                if at == UPAIRS - 1:
                    if not (isinstance(i, int) and i == 0 and u == 0):
                        dve.wait_ge(y_made.sem, y_made.after(i, UPAIRS * u))
                    set_cblk(i + (u + PARTS - 1) // UNITS, (u + PARTS - 1) % UNITS)

            def step(i, c, late):
                at_pair = [0]

                def scan(pairs):
                    for _ in range(pairs if i is not None else 0):
                        scan_pair(i, at_pair[0])
                        at_pair[0] += 1

                def ln_stats(c, k, src, done, n_done):
                    for tile in range(TILES):
                        dve.wait_ge(done.sem, done.after(c, n_done[tile]))
                        dve.bn_stats(stats[:, tile], src[:, tile]).then_inc(bn_done[k].sem, 1)
                    for tile in range(TILES):
                        wait_apart(bn_done[k], bn_done[k].after(c, tile + 1))
                        dve.bn_aggr(mv[:, k, tile], stats[:, tile]).then_inc(aggr_done[k].sem, 1)

                def ln_apply(c, k, src, dst, done):
                    dve.wait_ge(rstd_done[k].sem, rstd_done[k].after(c, 1))
                    for tile in range(TILES):
                        dve.tensor_scalar(dst[:, tile], src[:, tile], mv[:, k, tile, 0:1], rstd[:, k, tile:tile + 1],
                                          ALU.subtract, ALU.mult).then_inc(done.sem, 1)

                def ln_affine(k, src, scale, bias, dst, done):
                    dve.wait_ge(aggr_done[k].sem, aggr_done[k].after(c, TILES))
                    for tile in range(TILES):
                        dve.scalar_tensor_tensor(out=dst[:, tile], in0=src[:, tile], scalar=mv[:, k, tile, 0:1],
                                                 in1=rows[scale][:], op0=ALU.subtract, op1=ALU.mult).then_inc(u_done[k].sem, 1)
                    dve.wait_ge(rstd_done[k].sem, rstd_done[k].after(c, 1))
                    for tile in range(TILES):
                        dve.wait_ge(u_done[k].sem, u_done[k].after(c, tile + 1))
                        dve.scalar_tensor_tensor(out=dst[:, tile], in0=dst[:, tile], scalar=rstd[:, k, tile:tile + 1],
                                                 in1=bias(tile), op0=ALU.mult, op1=ALU.add).then_inc(done.sem, 1)

                def routing(c, f):
                    dve.wait_ge(gated[f].sem, gated[f].after(c, 1))
                    dve.tensor_tensor(score[:], TB[:, 0:TILES * E].rearrange("p (i e) -> p i e", i=TILES),
                                      g["gate_b"][:].unsqueeze(1).broadcast_to([P, TILES, E]), ALU.add).then_inc(route[f].sem, 1)
                    dve.wait_ge(route[f].sem, route[f].after(c, 1))
                    grid = [P, E, E]
                    steps = (
                        lambda i_, e_, f_, gt, ge: dve.tensor_tensor(gt, f_, e_, ALU.is_gt),
                        lambda i_, e_, f_, gt, ge: dve.tensor_tensor(ge, f_, e_, ALU.is_equal),
                        lambda i_, e_, f_, gt, ge: dve.tensor_tensor(ge, ge, g["before"][:].rearrange("p (e f) -> p e f", e=E), ALU.mult),
                        lambda i_, e_, f_, gt, ge: dve.tensor_tensor(gt, gt, ge, ALU.add),
                        lambda i_, e_, f_, gt, ge: dve.tensor_reduce(rank[:, i_], gt, AX.X, ALU.add),
                        lambda i_, e_, f_, gt, ge: dve.tensor_scalar(rank[:, i_], rank[:, i_], 1.5, None, ALU.is_lt),
                        lambda i_, e_, f_, gt, ge: dve.tensor_tensor(comb[:, f, i_], rank[:, i_], score[:, i_], ALU.mult),
                    )
                    for n, step in enumerate(steps):
                        for tile in range(TILES):
                            e_ = score[:, tile].unsqueeze(2).broadcast_to(grid)
                            f_ = score[:, tile].unsqueeze(1).broadcast_to(grid)
                            gt = above[:, tile].rearrange("p (e f) -> p e f", e=E)
                            ge = level[:, tile].rearrange("p (e f) -> p e f", e=E)
                            if n >= 2:
                                dve.wait_ge(route[f].sem, route[f].after(c, 1 + TILES * (n - 1) + tile + 1))
                            step(tile, e_, f_, gt, ge).then_inc(comb_done[f].sem if n == 6 else route[f].sem, 1)

                def set_acc(c, f, dst, src):
                    dve.wait_ge(bias_made[f].sem, bias_made[f].after(c, 1))
                    dve.tensor_tensor(dst[:].rearrange("p i d -> p (i d)"), TB[:], src[:].rearrange("p i d -> p (i d)"),
                                      ALU.add).then_inc(acc_set[f].sem, 1)

                def add_expert(c, f, e, dst):
                    dve.wait_ge(expert_out[f].sem, expert_out[f].after(c, e + 1))
                    if e == 0:
                        dve.wait_ge(acc_set[f].sem, acc_set[f].after(c, 1))
                        dve.wait_ge(comb_done[f].sem, comb_done[f].after(c, TILES))
                    for tile in range(TILES):
                        if e:
                            dve.wait_ge(acc_done[f].sem, acc_done[f].after(c, TILES * (e - 1) + tile + 1))
                        dve.scalar_tensor_tensor(out=dst[:, tile], in0=OB[(e + 1) % 2][:, tile * D:(tile + 1) * D],
                                                 scalar=comb[:, f, tile, e:e + 1], in1=dst[:, tile],
                                                 op0=ALU.mult, op1=ALU.add).then_inc(acc_done[f].sem, 1)

                def late_experts(first, end, scans):
                    for e in range(first, end):
                        scan(scans)
                        add_expert(late, 1, e, x3)

                scan(2)
                if c is not None:
                    dve.wait_ge(y_tposed.sem, y_tposed.after(c, 1))
                    dve.wait_ge(tok_in.sem, tok_in.after(c, 16 * 3 * B))
                    dve.tensor_tensor(z_t[:].rearrange("p k b t -> p k t b"), TB[:].rearrange("p (k t b) -> p k t b", k=KD, b=B),
                                      z_t[:].rearrange("p k b t -> p k t b"), ALU.mult).then_inc(y_gated.sem, 1)
                scan(1)
                if c is not None:
                    dve.wait_ge(mamba_out.sem, mamba_out.after(c, 1))
                    dve.wait_ge(xn_biased.sem, xn_biased.after(c, 1))
                    if late is not None:
                        dve.wait_ge(mb_done.sem, mb_done.after(late, 1))
                    dve.tensor_tensor(res[:].rearrange("p i d -> p (i d)"), OB[0][:], xn_t[:].rearrange("p i d -> p (i d)"),
                                      ALU.add).then_inc(h_done.sem, 1)
                    ln_stats(c, MAMBA, res, h_done, (1, 1))
                    dve.wait_ge(x_biased.sem, x_biased.after(c, 1))
                    ln_affine(MAMBA, res, "ln_w", lambda tile: x_t[:, tile], res, x1_done)
                    ln_stats(c, FFN1, res, x1_done, (1, 2))
                    ln_apply(c, FFN1, res, turn, xf_done[0])
                scan(3)
                if late is not None:
                    dve.wait_ge(mlp_made.sem, mlp_made.after(late, 1))
                    dve.wait_ge(mb_done.sem, mb_done.after(late, 2))
                    dve.wait_ge(stored.sem, stored.after(late, 0))
                    dve.tensor_tensor(x3[:].rearrange("p i d -> p (i d)"), OB[1][:], mb[:].rearrange("p i d -> p (i d)"),
                                      ALU.add).then_inc(x3_done.sem, 1)
                    ln_stats(late, FFN2, x3, x3_done, (1, 1))
                if c is not None:
                    routing(c, 0)
                scan(2)
                if c is not None:
                    set_acc(c, 0, res, res)
                for e in range(E):
                    if e:
                        scan(1)
                    if c is not None:
                        add_expert(c, 0, e, res)
                    if late is not None:
                        if e == 0:
                            ln_apply(late, FFN2, x3, late_turn, xf_done[1])
                        if e == GATE_AFTER:
                            routing(late, 1)
                        if e == BIAS_AFTER:
                            set_acc(late, 1, x3, x3)
                if c is not None:
                    ln_stats(c, OUTER, res, acc_done[0], (TILES * (E - 1) + 1, TILES * E))
                scan(1)
                if c is not None:
                    ln_apply(c, OUTER, res, a_t, a_done)
                    ln_stats(c, LN1, a_t, a_done, (1, 2))
                if late is not None:
                    late_experts(0, 1, 0)
                if c is not None:
                    ln_affine(LN1, a_t, "ln1_s", lambda tile: rows["ln1_b"][:], turn, xl_done)
                if late is not None:
                    late_experts(1, 2, 0)
                scan(1)
                if late is not None:
                    late_experts(2, 3, 1)
                    late_experts(3, 4, 0)
                if c is None:
                    if late is not None:
                        late_experts(4, 8, 1)
                    else:
                        scan(PAIRS - at_pair[0])
                    return
                scan(1)
                for bs, made, dst, done in ((HB, k_made, kT, kT_done), (OB, q_made, qT, qT_done)):
                    for j in range(2):
                        dve.wait_ge(made.sem, made.after(c, j + 1))
                        dve.tensor_scalar(dst[:, 2 * j:2 * j + 2].rearrange("p k q -> p (k q)"), bs[j][:], 0.0,
                                          g["feature_eps"][:, 0:1], ALU.max, ALU.add).then_inc(done.sem, 1)
                    if done is kT_done:
                        scan(1)
                for tile in range(TILES):
                    SB = (HB[0], HB[1], TB, OB[1])
                    if tile:
                        dve.wait_ge(num_made.sem, num_made.after(c, tile))
                    for hh in range(GH):
                        dve.wait_ge(scored.sem, scored.after(c, GH * tile + hh + 1))
                        dve.tensor_tensor(ss[:, hh], SB[hh][:].rearrange("p (g q) -> p g q", g=GROUPS),
                                          g["causal"][:].unsqueeze(1).broadcast_to([P, GROUPS, P]), ALU.mult).then_inc(masked.sem, 1)
                        if hh == 1:
                            scan(1)
                    scan(2)
                    dve.wait_ge(num_made.sem, num_made.after(c, tile + 1))
                    num = OB[0][:, 0:H * HV].rearrange("p (h v) -> p h v", h=H)
                    dve.reciprocal(rec[:, tile], num[:, :, DH]).then_inc(rec_done.sem, 1)
                    dve.wait_ge(rec_done.sem, rec_done.after(c, tile + 1))
                    dve.tensor_tensor(turn[:, tile].rearrange("p (h m) -> p h m", h=H), num[:, :, 0:DH],
                                      rec[:, tile].unsqueeze(2).broadcast_to([P, H, DH]), ALU.mult).then_inc(at_done.sem, 1)
                    for b in (2 * tile, 2 * tile + 1):
                        dve.wait_ge(kv_made.sem, kv_made.after(c, b + 1))
                        if b != 1:
                            dve.wait_ge(kv_added.sem, kv_added.after(c, max(b - 1, 0)))
                        dve.tensor_tensor(kvm[:, b % 2], HB[b % 2][:, 0:H * HV], g["own_head"][:], ALU.mult).then_inc(kv_masked.sem, 1)
                    if not tile:
                        scan(1)
                        if late is not None:
                            scan(2)
                            late_experts(4, 6, 0)
                scan(1)
                dve.wait_ge(wo_made.sem, wo_made.after(c, 1))
                dve.tensor_tensor(a_t[:].rearrange("p i d -> p (i d)"), OB[1][:], a_t[:].rearrange("p i d -> p (i d)"),
                                  ALU.add).then_inc(xr_done.sem, 1)
                ln_stats(c, LN2, a_t, xr_done, (1, 1))
                if late is not None:
                    scan(1)
                ln_affine(LN2, a_t, "ln2_s", lambda tile: rows["ln2_b"][:], late_turn, yl_done)
                if late is not None:
                    scan(1)
                    late_experts(6, 8, 0)
                if i is not None:
                    scan(PAIRS - at_pair[0])

            for u in range(PARTS - 1):
                set_cblk(0, u)
            step(0, None, None)
            step(1, 0, None)
            with dve.Fori(2, CHUNKS) as i:
                step(i, i - 1, i - 2)
            step(None, CHUNKS - 1, CHUNKS - 2)
            step(None, None, CHUNKS - 1)


def lay_out(x):
    def per_partition(v):
        return np.ascontiguousarray(np.asarray(v).reshape(-1, P).T)

    def blocks(w):
        w = np.asarray(w)
        return np.ascontiguousarray(w.reshape(-1, P, w.shape[1]).transpose(1, 0, 2))

    def row(v):
        return np.ascontiguousarray(np.broadcast_to(np.asarray(v).reshape(1, -1), (P, np.asarray(v).size)))

    def padded(w):
        w = np.asarray(w)
        full = np.zeros((D, H, PADH), w.dtype)
        full[:, :, :DH] = w
        return blocks(full.reshape(D, H * PADH))

    a = {k[len("L0_"):]: np.asarray(v) for k, v in x.items()}
    conv = a["attn_a_conv_w"][:, 0, :].reshape(KD, P, TAPS).transpose(1, 0, 2)
    a_log = np.tile(a["attn_a_A_log"].T, (B, 1))
    return {
        "x": a["attn_a_x"],
        "in_w": blocks(a["attn_a_in_w"].T), "in_b": per_partition(a["attn_a_in_b"]),
        "conv_w": np.ascontiguousarray(conv), "conv_b": per_partition(a["attn_a_conv_b"]),
        "b_w": blocks(a["attn_a_B_w"].T), "b_b": row(a["attn_a_B_b"]),
        "c_w": blocks(a["attn_a_C_w"].T), "c_b": a["attn_a_C_b"].reshape(-1, 1),
        "a_log": np.ascontiguousarray(a_log),
        "out_w": blocks(a["attn_a_out_w"].T), "out_b": row(a["attn_a_out_b"]),
        "ln_w": row(a["attn_a_ln_w"]), "ln_b": row(a["attn_a_ln_b"]),
        "ln1_s": row(a["attn_b_ln1_scale"]), "ln1_b": row(a["attn_b_ln1_bias"]),
        "ln2_s": row(a["attn_b_ln2_scale"]), "ln2_b": row(a["attn_b_ln2_bias"]),
        "mlp_b2": row(a["attn_b_b2"]),
        "wq": padded(a["attn_b_wq"]), "wk": padded(a["attn_b_wk"]),
        "wv": blocks(a["attn_b_wv"].reshape(D, D)), "wo": blocks(a["attn_b_wo"].reshape(D, D)),
        "m_w1": blocks(a["attn_b_w1"]), "m_b1": per_partition(a["attn_b_b1"]), "m_w2": blocks(a["attn_b_w2"]),
        "gate_w": blocks(a["ffn_gate_w"]), "gate_b": row(a["ffn_gate_b"]),
        "f_w1": np.ascontiguousarray(a["ffn_w1"].reshape(E, KD, P, F).transpose(2, 0, 1, 3)),
        "f_b1": np.ascontiguousarray(a["ffn_b1"].reshape(E, F // P, P).transpose(2, 0, 1)),
        "f_w2": np.ascontiguousarray(a["ffn_w2"].reshape(E, F // P, P, D).transpose(2, 0, 1, 3)),
        "f_b2": a["ffn_b2"],
        **constants(),
    }


def kernel(**inputs):
    import concourse.bacc as bacc
    from concourse.bass_utils import run_bass_kernel_spmd

    arrays = lay_out(inputs)
    nc = bacc.Bacc("TRN2", target_bir_lowering=False, num_devices=1)
    names = {n: nc.dram_tensor(f"in_{n}", a.shape, mybir.dt.from_np(a.dtype), kind="ExternalInput").ap()
             for n, a in arrays.items()}
    out = nc.dram_tensor("out_0", (B, L, D), mybir.dt.float32, kind="ExternalOutput").ap()
    build(nc, names, out)
    r = run_bass_kernel_spmd(nc, [{f"in_{n}": a for n, a in arrays.items()}], core_ids=[0])
    return r.results[0]["out_0"]
```
